# Optimizing a Trainium2 kernel written in Bass

```python
import numpy as np
import jax
import jax.numpy as jnp

def _softmax(x, axis=-1):
    return jax.nn.softmax(x, axis=axis)

def _gelu(x):
    return jax.nn.gelu(x, approximate=True)

def _silu(x):
    return jax.nn.silu(x)

def _sigmoid(x):
    return jax.nn.sigmoid(x)

def _layernorm(x, axis=-1, eps=1e-05):
    m = jnp.mean(x, axis=axis, keepdims=True)
    v = jnp.var(x, axis=axis, keepdims=True)
    return (x - m) / jnp.sqrt(v + eps)

def _scatter_add(tgt, idx, src, axis=0):
    return tgt.at[idx].add(src)

def _segment_sum(src, seg, n):
    return jax.ops.segment_sum(src, seg, n)
kernel_name = 'mk_gps_d1_gnn_r8_71651f'

def setup_inputs(seed: int=0):
    np.random.seed(seed)
    _w = jnp.asarray

    def _rec_inputs():
        import jax
        import jax.numpy as jnp
        _gk = jax.random.key(seed)
        x = -8.776e-05 + 1 * jax.random.normal(jax.random.fold_in(_gk, 1), (6250, 256), jnp.float32)
        src = jax.random.randint(jax.random.fold_in(_gk, 2), (100000,), 0, 6250, jnp.int32)
        dst = jnp.minimum((6250 * jax.random.uniform(jax.random.fold_in(_gk, 3), (100000,)) ** 2.0).astype(jnp.int32), 49999)
        _o = jnp.argsort(dst, stable=True)
        src = src[_o]
        dst = dst[_o]
        edge_type_8 = jax.random.randint(jax.random.fold_in(_gk, 12), (100000,), 0, 8, jnp.int32)
        node_type_4 = jax.random.randint(jax.random.fold_in(_gk, 13), (6250,), 0, 4, jnp.int32)
        return (x, src, dst, edge_type_8, node_type_4)
    x, src, dst, edge_type_8, node_type_4 = _rec_inputs()

    def _L0_gnn_setup():
        import jax, jax.numpy as jnp
        import numpy as np
        N_NODES = 2500
        N_EDGES = 40000
        IN_DIM = 256
        OUT_DIM = 256
        N_HEADS = 4
        D_K = OUT_DIM // N_HEADS
        N_NTYPES = 4
        N_RELS = 8
        SQRT_DK = float(np.sqrt(D_K))

        def _typed_matmul(x, W, node_type):
            all_t = jnp.einsum('ni,tio->tno', x, W)
            return all_t[node_type, jnp.arange(x.shape[0])]
        key = jax.random.key(seed)
        ks = jax.random.split(key, 12)
        xav = lambda k, shape, fan: jax.random.normal(k, shape, jnp.float32) * (1.0 / np.sqrt(fan))
        return {'h': jax.random.normal(ks[0], (N_NODES, IN_DIM), jnp.float32), 'k_linears': xav(ks[1], (N_NTYPES, IN_DIM, OUT_DIM), IN_DIM), 'q_linears': xav(ks[2], (N_NTYPES, IN_DIM, OUT_DIM), IN_DIM), 'v_linears': xav(ks[3], (N_NTYPES, IN_DIM, OUT_DIM), IN_DIM), 'a_linears': xav(ks[4], (N_NTYPES, OUT_DIM, OUT_DIM), OUT_DIM), 'relation_att': xav(ks[5], (N_RELS, N_HEADS, D_K, D_K), D_K), 'relation_msg': xav(ks[6], (N_RELS, N_HEADS, D_K, D_K), D_K), 'relation_pri': jnp.ones((N_RELS, N_HEADS), jnp.float32), 'skip': jnp.ones((N_NTYPES,), jnp.float32), 'node_type': jax.random.randint(ks[7], (N_NODES,), 0, N_NTYPES), 'etype': jnp.sort(jax.random.randint(ks[8], (N_EDGES,), 0, N_RELS)), 'row_idx': jax.random.randint(ks[9], (N_EDGES,), 0, N_NODES), 'col_idx': jax.random.randint(ks[10], (N_EDGES,), 0, N_NODES)}
    _L0_gnn_all = _L0_gnn_setup()
    _L0_gnn_in = {k: v for k, v in _L0_gnn_all.items() if k in ('k_linears', 'q_linears', 'v_linears', 'a_linears', 'relation_att', 'relation_msg', 'relation_pri', 'skip')}
    del _L0_gnn_all

    def _L0_mix_setup():
        import jax, jax.numpy as jnp
        import numpy as np
        NHEAD = 8
        ATT_EPS = 1e-06
        LN_EPS = 1e-05

        def _layernorm(x, g, b):
            mu = jnp.mean(x, axis=-1, keepdims=True)
            var = jnp.mean(jnp.square(x - mu), axis=-1, keepdims=True)
            return (x - mu) * jax.lax.rsqrt(var + LN_EPS) * g + b
        key = jax.random.key(seed)
        ks = jax.random.split(key, 7)
        N, L, C = (4, 2048, 256)
        s = 1.0 / np.sqrt(C)
        return {'x': jax.random.normal(ks[0], (N, L, C), jnp.float32), 'Wq': jax.random.normal(ks[1], (C, C), jnp.float32) * s, 'Wk': jax.random.normal(ks[2], (C, C), jnp.float32) * s, 'Wv': jax.random.normal(ks[3], (C, C), jnp.float32) * s, 'Wm': jax.random.normal(ks[4], (C, C), jnp.float32) * s, 'W1': jax.random.normal(ks[5], (2 * C, 2 * C), jnp.float32) * (1.0 / np.sqrt(2 * C)), 'W2': jax.random.normal(ks[6], (2 * C, C), jnp.float32) * (1.0 / np.sqrt(2 * C)), 'g1': jnp.ones((C,), jnp.float32), 'b1': jnp.zeros((C,), jnp.float32), 'g2': jnp.ones((C,), jnp.float32), 'b2': jnp.zeros((C,), jnp.float32)}
    _L0_mix_all = _L0_mix_setup()
    _L0_mix_in = {k: v for k, v in _L0_mix_all.items() if k in ('Wq', 'Wk', 'Wv', 'Wm', 'W1', 'W2', 'g1', 'b1', 'g2', 'b2')}
    del _L0_mix_all

    def _L0_ffn_setup():
        import jax, jax.numpy as jnp
        import numpy as np
        B, S, D = (8, 512, 256)
        H = 4 * D
        CAPACITY = 0.5
        key = jax.random.key(seed)
        ks = jax.random.split(key, 6)
        x = jax.random.normal(ks[0], (B, S, D), dtype=jnp.float32)
        attention_mask = jnp.zeros((B, 1, 1, S), dtype=jnp.float32)
        wr = jax.random.normal(ks[1], (D, 1), dtype=jnp.float32) * 0.02
        br = jnp.zeros((1,), dtype=jnp.float32)
        w1 = jax.random.normal(ks[2], (D, H), dtype=jnp.float32) * 0.02
        b1 = jnp.zeros((H,), dtype=jnp.float32)
        w2 = jax.random.normal(ks[3], (H, D), dtype=jnp.float32) * 0.02
        b2 = jnp.zeros((D,), dtype=jnp.float32)
        return {'x': x, 'attention_mask': attention_mask, 'wr': wr, 'br': br, 'w1': w1, 'b1': b1, 'w2': w2, 'b2': b2}
    _L0_ffn_all = _L0_ffn_setup()
    _L0_ffn_in = {k: v for k, v in _L0_ffn_all.items() if k in ('attention_mask', 'wr', 'br', 'w1', 'b1', 'w2', 'b2')}
    del _L0_ffn_all
    return {'x': x, 'src': src, 'dst': dst, 'edge_type_8': edge_type_8, 'node_type_4': node_type_4, 'L0_gnn_k_linears': _L0_gnn_in['k_linears'], 'L0_gnn_q_linears': _L0_gnn_in['q_linears'], 'L0_gnn_v_linears': _L0_gnn_in['v_linears'], 'L0_gnn_a_linears': _L0_gnn_in['a_linears'], 'L0_gnn_relation_att': _L0_gnn_in['relation_att'], 'L0_gnn_relation_msg': _L0_gnn_in['relation_msg'], 'L0_gnn_relation_pri': _L0_gnn_in['relation_pri'], 'L0_gnn_skip': _L0_gnn_in['skip'], 'L0_mix_Wq': _L0_mix_in['Wq'], 'L0_mix_Wk': _L0_mix_in['Wk'], 'L0_mix_Wv': _L0_mix_in['Wv'], 'L0_mix_Wm': _L0_mix_in['Wm'], 'L0_mix_W1': _L0_mix_in['W1'], 'L0_mix_W2': _L0_mix_in['W2'], 'L0_mix_g1': _L0_mix_in['g1'], 'L0_mix_b1': _L0_mix_in['b1'], 'L0_mix_g2': _L0_mix_in['g2'], 'L0_mix_b2': _L0_mix_in['b2'], 'L0_ffn_attention_mask': _L0_ffn_in['attention_mask'], 'L0_ffn_wr': _L0_ffn_in['wr'], 'L0_ffn_br': _L0_ffn_in['br'], 'L0_ffn_w1': _L0_ffn_in['w1'], 'L0_ffn_b1': _L0_ffn_in['b1'], 'L0_ffn_w2': _L0_ffn_in['w2'], 'L0_ffn_b2': _L0_ffn_in['b2']}

def reference(x, src, dst, edge_type_8, node_type_4, L0_gnn_k_linears, L0_gnn_q_linears, L0_gnn_v_linears, L0_gnn_a_linears, L0_gnn_relation_att, L0_gnn_relation_msg, L0_gnn_relation_pri, L0_gnn_skip, L0_mix_Wq, L0_mix_Wk, L0_mix_Wv, L0_mix_Wm, L0_mix_W1, L0_mix_W2, L0_mix_g1, L0_mix_b1, L0_mix_g2, L0_mix_b2, L0_ffn_attention_mask, L0_ffn_wr, L0_ffn_br, L0_ffn_w1, L0_ffn_b1, L0_ffn_w2, L0_ffn_b2):
    import jax
    import jax.numpy as jnp

    def _L0_gnn_ref(h, k_linears, q_linears, v_linears, a_linears, relation_att, relation_msg, relation_pri, skip, node_type, etype, row_idx, col_idx):
        import jax, jax.numpy as jnp
        import numpy as np
        N_NODES = 2500
        N_EDGES = 40000
        IN_DIM = 256
        OUT_DIM = 256
        N_HEADS = 4
        D_K = OUT_DIM // N_HEADS
        N_NTYPES = 4
        N_RELS = 8
        SQRT_DK = float(np.sqrt(D_K))

        def _typed_matmul(x, W, node_type):
            all_t = jnp.einsum('ni,tio->tno', x, W)
            return all_t[node_type, jnp.arange(x.shape[0])]
        n = h.shape[0]
        k = _typed_matmul(h, k_linears, node_type).reshape(n, N_HEADS, D_K)
        q = _typed_matmul(h, q_linears, node_type).reshape(n, N_HEADS, D_K)
        v = _typed_matmul(h, v_linears, node_type).reshape(n, N_HEADS, D_K)
        q_att = jnp.einsum('nhd,rhde->rnhe', q, relation_att)
        v_msg = jnp.einsum('nhd,rhde->rnhe', v, relation_msg)
        aw_q_edge = q_att[etype, col_idx]
        msg_edge = v_msg[etype, row_idx]
        attn_score = jnp.sum(aw_q_edge * k[row_idx], axis=-1)
        score = attn_score * (relation_pri[etype] / SQRT_DK)
        m = jax.ops.segment_max(score, col_idx, num_segments=n)
        ex = jnp.exp(score - m[col_idx])
        denom = jax.ops.segment_sum(ex, col_idx, num_segments=n)
        alpha = ex / denom[col_idx]
        agg = jax.ops.segment_sum(alpha[..., None] * msg_edge, col_idx, num_segments=n)
        agg = agg.reshape(n, OUT_DIM)
        out = _typed_matmul(agg, a_linears, node_type)
        out = jax.nn.sigmoid(skip)[node_type][:, None] * out
        return out

    def _L0_mix_ref(x, Wq, Wk, Wv, Wm, W1, W2, g1, b1, g2, b2):
        import jax, jax.numpy as jnp
        import numpy as np
        NHEAD = 8
        ATT_EPS = 1e-06
        LN_EPS = 1e-05

        def _layernorm(x, g, b):
            mu = jnp.mean(x, axis=-1, keepdims=True)
            var = jnp.mean(jnp.square(x - mu), axis=-1, keepdims=True)
            return (x - mu) * jax.lax.rsqrt(var + LN_EPS) * g + b
        N, L, C = x.shape
        H = NHEAD
        D = C // H
        q = (x @ Wq).reshape(N, L, H, D)
        k = (x @ Wk).reshape(N, L, H, D)
        v = (x @ Wv).reshape(N, L, H, D)
        Q = jax.nn.elu(q) + 1.0
        K = jax.nn.elu(k) + 1.0
        v = v / L
        KV = jnp.einsum('nshd,nshv->nhdv', K, v)
        Z = 1.0 / (jnp.einsum('nlhd,nhd->nlh', Q, K.sum(axis=1)) + ATT_EPS)
        msg = jnp.einsum('nlhd,nhdv,nlh->nlhv', Q, KV, Z) * L
        msg = msg.reshape(N, L, C) @ Wm
        msg = _layernorm(msg, g1, b1)
        h = jnp.concatenate([x, msg], axis=-1) @ W1
        h = jax.nn.relu(h) @ W2
        msg = _layernorm(h, g2, b2)
        return x + msg

    def _L0_ffn_ref(x, attention_mask, wr, br, w1, b1, w2, b2):
        import jax, jax.numpy as jnp
        import numpy as np
        B, S, D = (8, 512, 256)
        H = 4 * D
        CAPACITY = 0.5
        b, s, d = x.shape
        weights = (jnp.einsum('bsd,do->bso', x, wr) + br)[..., 0]
        k = max(1, int(CAPACITY * s))
        kk = k - 1 if k > 1 else 1
        _, idx = jax.lax.top_k(weights, k)
        sel_idx = idx[:, :kk]
        sel = jnp.take_along_axis(x, sel_idx[:, :, None], axis=1)
        h = jax.nn.gelu(jnp.einsum('bkd,dh->bkh', sel, w1) + b1)
        y = jnp.einsum('bkh,hd->bkd', h, w2) + b2
        w_sel = jnp.take_along_axis(weights, sel_idx, axis=1)
        y = y * w_sel[..., None]
        batch_idx = jnp.arange(b)[:, None]
        processed = jnp.zeros_like(x).at[batch_idx, sel_idx].set(y)
        return processed + x
    xn = _layernorm(x, axis=-1)
    x = x + _L0_gnn_ref(xn, L0_gnn_k_linears, L0_gnn_q_linears, L0_gnn_v_linears, L0_gnn_a_linears, L0_gnn_relation_att, L0_gnn_relation_msg, L0_gnn_relation_pri, L0_gnn_skip, node_type_4, edge_type_8, src, dst) + _L0_mix_ref(xn[None], L0_mix_Wq, L0_mix_Wk, L0_mix_Wv, L0_mix_Wm, L0_mix_W1, L0_mix_W2, L0_mix_g1, L0_mix_b1, L0_mix_g2, L0_mix_b2)[0]
    x = x + _L0_ffn_ref(_layernorm(x, axis=-1)[None], L0_ffn_attention_mask, L0_ffn_wr, L0_ffn_br, L0_ffn_w1, L0_ffn_b1, L0_ffn_w2, L0_ffn_b2)[0]
    return x

_drawn_inputs = setup_inputs


def setup_inputs(seed=0):
    import zlib

    import numpy as np

    out = dict(_drawn_inputs(seed))
    spreads = {'L0_gnn_relation_pri': (1.0, 0.6),
     'L0_gnn_skip': (1.0, 0.6),
     'L0_mix_g1': (1.0, 0.2),
     'L0_mix_b1': (0.0, 0.268),
     'L0_mix_g2': (1.0, 0.2),
     'L0_mix_b2': (0.0, 0.1),
     'L0_ffn_b1': (0.0, 0.8),
     'L0_ffn_b2': (0.0, 0.8)}
    factors = {'L0_ffn_wr': 7.318, 'L0_ffn_w1': 8.0, 'L0_ffn_w2': 7.966}
    for name, (base, spread) in spreads.items():
        noise = np.random.default_rng([zlib.crc32(name.encode()), seed]).standard_normal(out[name].shape)
        drawn = base * np.exp(spread * noise) if base else spread * noise
        out[name] = jnp.asarray(drawn.astype(out[name].dtype))
    for name, factor in factors.items():
        out[name] = (out[name] * factor).astype(out[name].dtype)
    return out
```

```python
import numpy as np
import concourse.bass as bass
from concourse import mybir

f32, i32, i16, bf16 = mybir.dt.float32, mybir.dt.int32, mybir.dt.int16, mybir.dt.bfloat16
ALU = mybir.AluOpType
ACT = mybir.ActivationFunctionType
AX = mybir.AxisListType

P = 128
N, E, C = 6250, 100000, 256
NT = -(-N // P)
NP = NT * P
LAST = N - (NT - 1) * P
GT = 4
NG = -(-NT // GT)
CC = C // P
H, DK = 4, 64
R, T = 8, 4
GT2 = 2
TW = GT2 * P
CH = 256
HALF = CH // P
NCH = E // CH + (1 if E % CH else 0) + NT - 1
CG = -(-NCH // P)
NCP = CG * P
EP, EF = 125, 800
EPAD = E + CH
BIG = 1e30
LN_EPS, ATT_EPS = 1e-5, 1e-6
FF = 4 * C
FC = FF // P
KK = int(0.5 * N) - 1
AW = C + H


def tiles_of(g):
    return list(range(g * GT, min(NT, (g + 1) * GT)))


class Engine:

    def __init__(self, nc, eng, name):
        self.e, self.sem, self.count, self.seen = eng, nc.alloc_semaphore("done_" + name), 0, {}

    def need(self, *tokens):
        for tok in tokens:
            if tok is None:
                continue
            sem, value = tok
            if self.seen.get(id(sem), 0) < value:
                self.e.wait_ge(sem, value)
                self.seen[id(sem)] = value

    def mark(self, ins):
        self.count += 1
        ins.then_inc(self.sem, 1)
        return (self.sem, self.count)


class Slot:

    def __init__(self, nc, name):
        self.sem, self.value, self.last = nc.alloc_semaphore("dma_" + name), 0, None

    def start(self, eng, ins_of, *tokens):
        eng.need(self.last, *tokens)
        self.value += 16
        ins_of().then_inc(self.sem, 16)
        self.last = (self.sem, self.value)
        return self.last


class Banks:

    def __init__(self, banks):
        self.banks, self.free, self.at = banks, [None] * len(banks), -1

    def take(self, pe):
        self.at = (self.at + 1) % len(self.banks)
        pe.need(self.free[self.at])
        return self.at, self.banks[self.at]


def sort_edges(nc, d_dst, d_row, d_sorted, d_place, d_total, room, iota_row, iota_p, pool, unsorted, *ready):
    G = nc.gpsimd
    BLOCKS = -(-E // P)
    NODES = NP + P
    NF = NODES // P
    work, dma = nc.alloc_semaphore("sort_work"), nc.alloc_semaphore("sort_dma")
    lo = 0

    def part(*shape, dt=None):
        nonlocal lo
        n = int(np.prod(shape))
        ap = room[:, lo:lo + n]
        lo += n
        ap = ap if dt is None else ap.bitcast(dt)
        return ap if len(shape) == 1 else ap.rearrange("p (a b) -> p a b", a=shape[0])

    before, same = part(P), part(2, P)
    other, places, places2 = part(P), part(NF), part(NF)
    d_col, r_col, node, place, moved, target = (part(1) for _ in range(6))
    node_i, target_i = part(1, dt=i32), part(1, dt=i32)
    assert lo <= room.shape[1]

    def step(ins):
        ins.then_inc(work, 1)
        G.wait_ge(work, 1)
        G.sem_clear(work)

    def move(*dmas):
        for i, ins_of in enumerate(dmas):
            ins_of().then_inc(dma, 16)
            G.wait_ge(dma, 16 * (i + 1))
        G.dma_reset(range(dma.num, dma.num + 1))
        G.sem_clear(dma)

    def at_index(i):
        return bass.IndirectOffsetOnAxis(ap=i, axis=0)

    def blocks(put):
        with G.Fori(0, BLOCKS * P, P) as e0:
            move(lambda: G.dma_start(d_col, d_dst[bass.ds(e0, P), :]),
                 lambda: G.dma_start(other, d_dst[bass.ds(e0, P), :].rearrange("(o e) u -> o (e u)", o=1).to_broadcast([P, P])))
            step(G.tensor_scalar(same[:, 0, :], other, d_col, None, ALU.is_equal))
            step(G.tensor_tensor(out=same[:, 1, :], in0=same[:, 0, :], in1=before, op=ALU.mult))
            w = P // 2
            while w:
                step(G.tensor_tensor(out=same[:, :, 0:w], in0=same[:, :, 0:w], in1=same[:, :, w:2 * w], op=ALU.add))
                w //= 2
            step(G.tensor_scalar(node, d_col, float(NP), None, ALU.min))
            step(G.tensor_copy(node_i, node))
            move(lambda: G.indirect_dma_start(place, None, d_place[:, :], at_index(node_i)))
            step(G.tensor_tensor(out=moved, in0=place, in1=same[:, 0, 0:1], op=ALU.add))
            move(lambda: G.indirect_dma_start(d_place[:, :], at_index(node_i), moved, None))
            if put:
                step(G.tensor_tensor(out=target, in0=place, in1=same[:, 1, 0:1], op=ALU.add))
                step(G.tensor_copy(target_i, target))
                move(lambda: G.dma_start(r_col, d_row[bass.ds(e0, P), :]),
                     lambda: G.indirect_dma_start(d_sorted[0][:, :], at_index(target_i), d_col, None),
                     lambda: G.indirect_dma_start(d_sorted[1][:, :], at_index(target_i), r_col, None))

    pool.need(*ready)
    flag = nc.values_load(unsorted[0:1, 0:1], engines=[mybir.EngineType.Pool], min_val=0, max_val=E,
                          skip_runtime_bounds_check_because="it is a count of edges")
    with G.If(flag > 0):
        step(G.tensor_scalar(before, iota_row, iota_p, None, ALU.is_lt))
        step(G.memset(places, 0.0))
        move(lambda: G.dma_start(d_place.rearrange("(p f) u -> p (f u)", p=P), places))
        blocks(False)
        move(lambda: G.dma_start(places, d_place.rearrange("(p f) u -> p (f u)", p=P)))
        step(G.memset(places2[:, 0:1], 0.0))
        step(G.tensor_copy(places2[:, 1:NF], places[:, 0:NF - 1]))
        step(G.tensor_copy(moved, places[:, NF - 1:NF]))
        a, b, w = places2, places, 1
        while w < NF:
            step(G.tensor_copy(b[:, 0:w], a[:, 0:w]))
            step(G.tensor_tensor(out=b[:, w:NF], in0=a[:, w:NF], in1=a[:, 0:NF - w], op=ALU.add))
            a, b, w = b, a, 2 * w
        step(G.tensor_tensor(out=moved, in0=moved, in1=a[:, NF - 1:NF], op=ALU.add))
        move(lambda: G.dma_start(d_total[:, :], moved),
             lambda: G.dma_start(other, d_total.rearrange("(o e) u -> o (e u)", o=1).to_broadcast([P, P])))
        step(G.tensor_tensor(out=other, in0=other, in1=before, op=ALU.mult))
        w = P // 2
        while w:
            step(G.tensor_tensor(out=other[:, 0:w], in0=other[:, 0:w], in1=other[:, w:2 * w], op=ALU.add))
            w //= 2
        step(G.tensor_scalar(a, a, other[:, 0:1], None, ALU.add))
        move(lambda: G.dma_start(d_place.rearrange("(p f) u -> p (f u)", p=P), a))
        blocks(True)
        n = BLOCKS * P
        for i, d in enumerate((d_dst, d_row)):
            move(lambda: G.dma_start(d[0:n, :].rearrange("(p f) u -> p (f u)", p=P), d_sorted[i][0:n, :].rearrange("(p f) u -> p (f u)", p=P)))


def build(nc, x, src, dst, etype, ntype, kW, qW, vW, aW, att, msg, pri, skip, mWq, mWk, mWv, mWm,
          mW1, mW2, g1, b1, g2, b2, wr, br, fw1, fb1, fw2, fb2, out):
    pe, act, dve = Engine(nc, nc.tensor, "pe"), Engine(nc, nc.scalar, "act"), Engine(nc, nc.vector, "dve")
    pool, sp = Engine(nc, nc.gpsimd, "pool"), Engine(nc, nc.sync, "sp")
    V, A, G, TE = nc.vector, nc.scalar, nc.gpsimd, nc.tensor

    d_dst = nc.dram_tensor("edge_dst", (EPAD, 1), f32)
    d_row = nc.dram_tensor("edge_row", (EPAD, 1), f32)
    d_sorted = [nc.dram_tensor("sorted_" + q, (EPAD, 1), f32) for q in ("dst", "row")]
    d_place = nc.dram_tensor("next_place", (NP + P, 1), f32)
    d_total = nc.dram_tensor("block_total", (P, 1), f32)
    d_rel = nc.dram_tensor("chunk_rel", (NCP, CH), bf16)
    d_off = nc.dram_tensor("chunk_off", (2, NCP), i16)
    d_base = nc.dram_tensor("base", (NP, C), f32)
    d_ktab = nc.dram_tensor("k_table", (NP * R, C), f32)
    d_vtab = nc.dram_tensor("v_table", (NP * R, C), f32)

    ARENA, E_SIZE = 53200, 5400
    arena = nc.alloc_sbuf_tensor("arena", [P, ARENA], f32)
    at = [0]

    def room(n):
        lo = at[0]
        at[0] += n
        assert at[0] <= ARENA, at[0]
        return lo

    def view(lo, n, pat=None, dt=None, **kw):
        ap = arena[:, lo:lo + n]
        if dt is not None:
            ap = ap.bitcast(dt)
        return ap.rearrange(pat, **kw) if pat else ap

    xT = view(room(CC * NP), CC * NP, "p (c n) -> p c n", c=CC)
    lo_big = room((NT + 1) * AW)
    q_all = view(lo_big, (NT + 1) * C)
    acc = view(lo_big, (NT + 1) * AW)
    lo_S = room(H * NCP * HALF)
    S_all = view(lo_S, H * NCP * HALF, "p (h g j c) -> p h g j c", h=H, g=CG, j=HALF)
    S_row = view(lo_S, H * NCP * HALF, "p (h g e) -> p h g e", h=H, g=CG)
    relE = view(room(HALF * NCP // 2), HALF * NCP // 2, "p (g j c) -> p g j c", dt=bf16, g=CG, j=HALF)
    idxE = view(room(HALF * NCP), HALF * NCP, "p (g j c) -> p g j c", dt=i32, g=CG, j=HALF)
    ident, iota_row, ones = view(room(P), P), view(room(P), P), view(room(P), P)
    iota_p = view(room(1), 1)
    lo_flag = room(CG * (CH + 2) // 2)
    flag = view(lo_flag, CG * (CH + 2) // 2, "p (g e) -> p g e", dt=bf16, g=CG)
    offr = view(room(NCP), NCP, dt=i16)[0:1, :]
    lo_cr = room(4 * (NCP // 2))
    small = room(1000)
    lo_E = room(E_SIZE)
    lo_B = room(ARENA - at[0])
    B_SIZE = ARENA - lo_B

    banks = [nc.alloc_psum_tensor(f"bank{i}", [P, 512], f32) for i in range(8)]
    fg, bg = Banks(banks[0:3]), Banks(banks[3:6])
    allb = Banks(banks[0:6])

    t_io = pool.mark(G.iota(iota_row, [[1, P]], base=0, channel_multiplier=0, allow_small_or_imprecise_dtypes=True))
    t_ip = pool.mark(G.iota(iota_p, [[1, 1]], base=0, channel_multiplier=1, allow_small_or_imprecise_dtypes=True))
    dve.need(t_io, t_ip)
    t_id = dve.mark(V.tensor_scalar(ident, iota_row, iota_p, None, ALU.is_equal))
    t_one = dve.mark(V.memset(ones, 1.0))

    def transpose(dst_ps, src_ap):
        return TE.transpose(dst_ps, src_ap, ident)

    def rsqrt(eng_vars, y, tmp, n, tok):
        dve.need(tok)
        t = dve.mark(V.tensor_scalar(y.bitcast(i32), eng_vars.bitcast(i32), -0.5, float(0x5F3759DF), ALU.mult, ALU.add))
        for _ in range(4):
            dve.need(t)
            t = dve.mark(V.tensor_tensor(out=tmp, in0=y, in1=y, op=ALU.mult))
            dve.need(t)
            t = dve.mark(V.tensor_tensor(out=tmp, in0=tmp, in1=eng_vars, op=ALU.mult))
            dve.need(t)
            t = dve.mark(V.tensor_scalar(tmp, tmp, -0.5, 1.5, ALU.mult, ALU.add))
            dve.need(t)
            t = dve.mark(V.tensor_tensor(out=y, in0=y, in1=tmp, op=ALU.mult))
        return t

    sm = [small]

    def tiny(n, dt=None):
        lo = sm[0]
        sm[0] += n
        assert sm[0] <= small + 1000
        ap = arena[:, lo:lo + n]
        return ap if dt is None else ap.bitcast(dt)

    stats = tiny(GT * 6).rearrange("p (t s) -> p t s", s=6)
    mv = tiny(GT * 2).rearrange("p (t s) -> p t s", s=2)
    var, rstd, nt_tmp = tiny(GT), tiny(GT), tiny(GT)
    g1T, b1T = tiny(CC), tiny(CC)
    priP = tiny(CC * R).rearrange("p (c r) -> p c r", c=CC)
    fb1T = tiny(FC)
    skipP = tiny(T)
    brP = tiny(1)
    wrT = tiny(CC)

    def ln_stats(tile_aps, tok):
        n = len(tile_aps)
        dve.need(tok)
        ts = []
        for i, ap in enumerate(tile_aps):
            ts.append(dve.mark(V.bn_stats(stats[:, i, :], ap)))
        for i in range(n):
            dve.need(ts[i])
            t = dve.mark(V.bn_aggr(mv[:, i, :], stats[:, i, :]))
        dve.need(t)
        t = dve.mark(V.tensor_scalar(var[:, 0:n], mv[:, 0:n, 1], LN_EPS, None, ALU.add))
        return rsqrt(var[:, 0:n], rstd[:, 0:n], nt_tmp[:, 0:n], n, t)

    s_small = [Slot(nc, f"small{i}") for i in range(8)]
    nsm = [0]

    def load_small(dst_ap, src_ap, *tok):
        nsm[0] += 1
        return s_small[nsm[0] % 8].start(sp, lambda: nc.sync.dma_start(dst_ap, src_ap, allow_slow_non_contiguous=True), *tok)

    lo = lo_B
    Wt = view(lo, T * CC * C, "p (t c n) -> p t c n", t=T, c=CC); lo += T * CC * C
    BD = view(lo, CC * R * P, "p (c r n) -> p c r n", c=CC, r=R); lo += CC * R * P
    lo_M = lo
    M = view(lo, T * CC * TW, "p (t c n) -> p t c n", t=T, c=CC); lo += T * CC * TW
    zT = view(lo, CC * TW, "p (c n) -> p c n", c=CC); lo += CC * TW
    tabs = [view(lo + i * R * C, R * C, "p (r n) -> p r n", r=R) for i in range(2)]; lo += 2 * R * C
    ntr = [view(lo + i * TW, TW, dt=i32) for i in range(2)]; lo += 2 * TW
    assert lo <= lo_B + B_SIZE
    Wq = view(lo_S, T * CC * C, "p (t c n) -> p t c n", t=T, c=CC)

    lo = lo_E
    NX = 3
    xs = [view(lo + i * GT * C, GT * C, "p (t n) -> p t n", t=GT) for i in range(NX)]; lo += NX * GT * C
    xns = [view(lo + i * GT * C, GT * C, "p (t n) -> p t n", t=GT) for i in range(2)]; lo += 2 * GT * C
    b2row = view(lo, C); lo += C
    assert lo <= lo_E + E_SIZE

    sx = [Slot(nc, f"x{i}") for i in range(NX)]
    sbase = [Slot(nc, f"base{i}") for i in range(2)]

    t_zero = dve.mark(V.memset(xs[(NG - 1) % NX][:, :, :], 0.0))
    t_b2 = load_small(b2row, b2.rearrange("(o n) -> o n", o=1).to_broadcast([P, C]))
    x_free = [None] * NX
    x_free[(NG - 1) % NX] = t_zero

    def load_x(g):
        i = g % NX
        ts = tiles_of(g)
        if g < NG - 1:
            return sx[i].start(sp, lambda: nc.sync.dma_start(
                xs[i][:, 0:len(ts), :], x[g * 512:g * 512 + len(ts) * P, :].rearrange("(t p) n -> p t n", p=P)), x_free[i])
        return sx[i].start(sp, lambda: nc.sync.dma_start(xs[i][0:LAST, 0, :], x[g * 512:N, :]), x_free[i])

    tx = [None] * NG
    for g in range(NX):
        tx[g] = load_x(g) if not (g == (NG - 1) % NX) else sx[g].start(sp, lambda: nc.sync.dma_start(
            xs[g][:, :, :], x[g * 512:(g + 1) * 512, :].rearrange("(t p) n -> p t n", p=P)), t_zero)
    t_Wk = [load_small(Wt[:, t, :, :], kW[t].rearrange("(c p) n -> p c n", p=P)) for t in range(T)]
    t_Wq = [load_small(Wq[:, t, :, :], qW[t].rearrange("(c p) n -> p c n", p=P)) for t in range(T)]
    xn_free = [None, None]
    pe_read = [None, None]
    t_xT = [None] * NG
    for g in range(NG):
        ts = tiles_of(g)
        n = len(ts)
        xb, xnb = xs[g % NX], xns[g % 2]
        if g == NG - 1:
            dve.need(x_free[g % NX])
            tz = dve.mark(V.memset(xb[:, 0, :], 0.0))
            x_free[g % NX] = tz
            tx[g] = load_x(g)
        t = ln_stats([xb[:, i, :] for i in range(n)], tx[g])
        dve.need(t, xn_free[g % 2], pe_read[g % 2])
        for i in range(n):
            t = dve.mark(V.tensor_scalar(xnb[:, i, :], xb[:, i, :], mv[:, i, 0:1], rstd[:, i:i + 1], ALU.subtract, ALU.mult))
        pe.need(t, t_id)
        for c in range(CC):
            k, bank = allb.take(pe)
            for i in range(n):
                ins = transpose(bank[:, i * P:(i + 1) * P], xnb[:, i, c * P:(c + 1) * P])
            tp = pe.mark(ins)
            act.need(tp)
            t_xT[g] = allb.free[k] = act.mark(A.copy(xT[:, c, g * 512:g * 512 + n * P], bank[:, 0:n * P]))
        pe_read[g % 2] = tp
        pool.need(t, t_b2)
        tb = pool.mark(G.tensor_tensor(out=xb[:, 0:n, :], in0=xb[:, 0:n, :], in1=xnb[:, 0:n, :], op=ALU.add))
        xn_free[g % 2] = tb
        pool.need(tb)
        tb = pool.mark(G.tensor_tensor(out=xb[:, 0:n, :], in0=xb[:, 0:n, :],
                                       in1=b2row.unsqueeze(1).to_broadcast([P, n, C]), op=ALU.add))
        x_free[g % NX] = sbase[g % 2].start(sp, lambda: nc.sync.dma_start(
            d_base[g * 512:g * 512 + n * P, :].rearrange("(t p) n -> p t n", p=P), xb[:, 0:n, :]), tb)
        if g + NX < NG - 1:
            tx[g + NX] = load_x(g + NX)
    t_base_all = [s.last for s in sbase]
    E_free = [xn_free[0], xn_free[1], tp] + t_base_all

    def load_blocks(rel, *tok):
        dve.need(*tok)
        tz = dve.mark(V.memset(BD[:, :, :, :], 0.0))
        toks = []
        for c in range(CC):
            for h2 in range(2):
                toks.append(load_small(BD[h2 * DK:(h2 + 1) * DK, c, :, h2 * DK:(h2 + 1) * DK],
                                       rel[:, 2 * c + h2, :, :].rearrange("r d e -> d r e"), tz))
        return toks

    tb4 = load_blocks(att)
    for c in range(CC):
        for h2 in range(2):
            t_pri = load_small(priP[h2 * DK:(h2 + 1) * DK, c, :],
                               pri.rearrange("r (h o) -> h o r", o=1)[2 * c + h2].to_broadcast([DK, R]))
            tb4.append(t_pri)
    pe.need(*tb4)
    for c in range(CC):
        for r0 in range(0, R, 4):
            k, bank = allb.take(pe)
            for r in range(r0, r0 + 4):
                ins = transpose(bank[:, (r - r0) * P:(r - r0 + 1) * P], BD[:, c, r, :])
            tp = pe.mark(ins)
            dve.need(tp, *tb4)
            for r in range(r0, r0 + 4):
                t_att = dve.mark(V.tensor_scalar(BD[:, c, r, :], bank[:, (r - r0) * P:(r - r0 + 1) * P],
                                                 priP[:, c, r:r + 1], float(1.0 / np.sqrt(DK)), ALU.mult, ALU.mult))
            allb.free[k] = t_att

    s_nt = [Slot(nc, f"ntype{i}") for i in range(2)]
    s_tab = [Slot(nc, f"table{i}") for i in range(2)]
    tab_last = []

    def make_table(bk, table, t_w, with_q, t_free, evac, steps):
        nt_free, m_free, z_free, tab_free = [None, None], t_free, None, [None, None]
        k_tile = 0
        for g in range(-(-NT // GT2)):
            n = min(GT2, NT - g * GT2)
            w = n * P
            valid = min(N - g * TW, w)
            row = ntr[g % 2]
            tn = s_nt[g % 2].start(sp, lambda: nc.sync.dma_start(
                row[:, 0:valid], ntype[g * TW:g * TW + valid].rearrange("(o n) -> o n", o=1).to_broadcast([P, valid])), nt_free[g % 2])
            if valid < w:
                dve.need(nt_free[g % 2])
                tm = dve.mark(V.memset(row[:, valid:w], 0))
                dve.need(tm)
            dve.need(tn, t_xT[g * GT2 // GT], m_free)
            for t in range(T):
                tm = dve.mark(V.scalar_tensor_tensor(
                    out=M[:, t, :, 0:w], in0=row[:, 0:w].unsqueeze(1).to_broadcast([P, CC, w]), scalar=float(t),
                    in1=xT[:, :, g * TW:g * TW + w], op0=ALU.is_equal, op1=ALU.mult))
            nt_free[g % 2] = tm
            yield
            pe.need(tm, *t_w)
            for oc in range(CC):
                k, bank = bk.take(pe)
                for i in range(T * CC):
                    t, c = divmod(i, CC)
                    ins = TE.matmul(bank[:, 0:w], lhsT=Wt[:, t, c, oc * P:(oc + 1) * P], rhs=M[:, t, c, 0:w],
                                    start=i == 0, stop=i == T * CC - 1)
                    if i == 3 and steps:
                        yield
                tp = pe.mark(ins)
                act.need(tp, z_free)
                tz = bk.free[k] = act.mark(A.copy(zT[:, oc, 0:w], bank[:, 0:w]))
            if with_q:
                for i4 in range(n):
                    k, bank = bk.take(pe)
                    for i in range(T * CC):
                        t, c = divmod(i, CC)
                        ins = TE.matmul(bank[:, 0:C], lhsT=M[:, t, c, i4 * P:(i4 + 1) * P], rhs=Wq[:, t, c, :],
                                        start=i == 0, stop=i == T * CC - 1)
                    tp = pe.mark(ins)
                    act.need(tp)
                    t_q = bk.free[k] = act.mark(A.copy(q_all[:, (g * GT2 + i4) * C:(g * GT2 + i4 + 1) * C], bank[:, 0:C]))
            m_free = tp
            yield
            pe.need(tz)
            for i4 in range(n):
                tile = g * GT2 + i4
                tb = tabs[k_tile % 2]
                te = []
                for c in range(CC):
                    for half in range(2):
                        k, bank = bk.take(pe)
                        tp = pe.mark(TE.matmul(bank[:, :], lhsT=zT[:, c, i4 * P:(i4 + 1) * P],
                                               rhs=BD[:, c, half * 4:half * 4 + 4, :], start=True, stop=True))
                        o, i_ = tb[:, half * 4:half * 4 + 4, c * P:(c + 1) * P], bank[:, :].rearrange("p (r n) -> p r n", r=4)
                        if evac == "both" and half:
                            dve.need(tp, tab_free[k_tile % 2])
                            t_e = dve.mark(V.tensor_copy(o, i_))
                        else:
                            act.need(tp, tab_free[k_tile % 2])
                            t_e = act.mark(A.copy(o, i_))
                        bk.free[k] = t_e
                        te.append(t_e)
                    if steps:
                        yield
                tab_free[k_tile % 2] = s_tab[k_tile % 2].start(sp, lambda: nc.sync.dma_start(
                    table[tile * P * R:(tile + 1) * P * R, :].rearrange("(p r) n -> p (r n)", r=R),
                    tb.rearrange("p r n -> p (r n)")), *te)
                k_tile += 1
                yield
            z_free = tp
        tab_last[:] = [tab_free[0], tab_free[1], m_free, z_free, nt_free[0], nt_free[1], tm]
        if with_q:
            tab_last.append(t_q)

    lo = lo_E
    ed_i = view(lo, EF, dt=i32)[0:EP, :]; lo += EF
    ed = view(lo, EF)[0:EP, :]; lo += EF
    es_i = view(lo, EF, dt=i32)[0:EP, :]; lo += EF
    et_i = view(lo, EF, dt=i32)[0:EP, :]; lo += EF
    junk = view(lo, EF // 2, dt=bf16)[0:EP, :]; lo += EF // 2
    cnt = view(lo, NT + 1)[0:EP, :]; lo += NT + 1
    nxt_i, nxt = view(lo, 1, dt=i32)[0:EP, :], view(lo + 1, 1)[0:EP, :]; lo += 2
    lo_sort = lo
    t_d = load_small(ed_i, dst.rearrange("(p f) -> p f", p=EP), *E_free)
    t_s = load_small(es_i, src.rearrange("(p f) -> p f", p=EP), *E_free)
    t_t = load_small(et_i, etype.rearrange("(p f) -> p f", p=EP), *E_free)
    dve.need(*E_free)
    t = dve.mark(V.memset(nxt_i, 2 ** 24))
    t_n = load_small(nxt_i[0:EP - 1, :], dst.rearrange("(p f) -> p f", p=EP)[1:EP, 0:1], t)
    dve.need(t_d, t_s, t_t, t_n)
    t = dve.mark(V.tensor_copy(nxt, nxt_i))
    t = dve.mark(V.tensor_copy(ed, ed_i))
    dve.need(t)
    t = dve.mark(V.tensor_tensor(out=junk[:, 0:EF - 1], in0=ed[:, 1:EF], in1=ed[:, 0:EF - 1], op=ALU.is_lt))
    t = dve.mark(V.tensor_tensor(out=junk[:, EF - 1:EF], in0=nxt, in1=ed[:, EF - 1:EF], op=ALU.is_lt))
    dve.need(t)
    t = dve.mark(V.tensor_reduce(cnt[:, NT:NT + 1], junk, AX.X, ALU.add))
    t_er = dve.mark(V.scalar_tensor_tensor(out=ed_i.bitcast(f32), in0=es_i, scalar=float(R), in1=et_i, op0=ALU.mult, op1=ALU.add))
    tw = [load_small(d_dst[0:E, :].rearrange("(p f) o -> p (f o)", p=EP), ed, t),
          load_small(d_row[0:E, :].rearrange("(p f) o -> p (f o)", p=EP), ed_i.bitcast(f32), t_er)]
    padv = tiny(4)
    t1 = dve.mark(V.memset(padv[:, 0:2], float(4 * NP)))
    t2 = dve.mark(V.memset(padv[:, 2:4], 0.0))
    tw.append(load_small(d_dst[E:EPAD, :].rearrange("(p f) o -> p (f o)", p=P), padv[:, 0:2], t1))
    tw.append(load_small(d_row[E:EPAD, :].rearrange("(p f) o -> p (f o)", p=P), padv[:, 2:4], t2))
    tc_ = t
    for b in range(NT):
        dve.need(tc_)
        tc_ = dve.mark(V.tensor_scalar(junk, ed, float(P * (b + 1)), None, ALU.is_lt, ALU.add, accum_out=cnt[:, b:b + 1]))
    NB = NT
    edge_end = tiny(NB)
    n_edge, n_chunk, chunk_end = tiny(NB), tiny(NB), tiny(NB)
    nci = tiny(NB, i32)
    pe.need(tc_, t_one)
    k, bank = allb.take(pe)
    tp = pe.mark(TE.matmul(bank[:, 0:NB + 1], lhsT=ones[0:EP, :], rhs=cnt, start=True, stop=True))
    dve.need(tp)
    unsorted = tiny(1, i32)
    t_uns = dve.mark(V.tensor_copy(unsorted, bank[:, NB:NB + 1]))
    t = allb.free[k] = dve.mark(V.tensor_copy(edge_end, bank[:, 0:NB]))
    dve.need(t)
    t = dve.mark(V.tensor_copy(n_edge[:, 0:1], edge_end[:, 0:1]))
    t = dve.mark(V.tensor_tensor(out=n_edge[:, 1:NB], in0=edge_end[:, 1:NB], in1=edge_end[:, 0:NB - 1], op=ALU.subtract))
    dve.need(t)
    t = dve.mark(V.tensor_scalar(nci, n_edge, float(CH - 1), None, ALU.add))
    dve.need(t)
    t = dve.mark(V.tensor_scalar(nci, nci, int(np.log2(CH)), None, ALU.arith_shift_right))
    dve.need(t)
    t = dve.mark(V.tensor_copy(n_chunk, nci))
    dve.need(t)
    t = dve.mark(V.tensor_tensor_scan(out=chunk_end, data0=n_chunk, data1=n_chunk, initial=0.0, op0=ALU.add, op1=ALU.bypass))
    iota_c, c_tile, c_e0, c_c0 = tiny(CG), tiny(CG), tiny(CG), tiny(CG)
    start_i = tiny(CG, i32)
    offs = tiny(CG, i16).rearrange("p (o g) -> p o g", o=2)
    cmp_, pr = tiny(NB), tiny(NB)
    t_ic = pool.mark(G.iota(iota_c, [[P, CG]], base=0, channel_multiplier=1, allow_small_or_imprecise_dtypes=True))
    dve.need(t, t_ic)
    for g in range(CG):
        t = dve.mark(V.tensor_scalar(cmp_, chunk_end, iota_c[:, g:g + 1], None, ALU.is_le))
        dve.need(t)
        t = dve.mark(V.tensor_reduce(c_tile[:, g:g + 1], cmp_, AX.X, ALU.add))
        for q, o in ((n_edge, c_e0), (n_chunk, c_c0)):
            dve.need(t)
            t = dve.mark(V.tensor_tensor(out=pr, in0=cmp_, in1=q, op=ALU.mult))
            dve.need(t)
            t = dve.mark(V.tensor_reduce(o[:, g:g + 1], pr, AX.X, ALU.add))
        dve.need(t)
    t = dve.mark(V.tensor_tensor(out=c_c0, in0=iota_c, in1=c_c0, op=ALU.subtract))
    dve.need(t)
    t = dve.mark(V.tensor_scalar(c_c0, c_c0, float(CH), None, ALU.mult))
    dve.need(t)
    t = dve.mark(V.tensor_tensor(out=c_c0, in0=c_c0, in1=c_e0, op=ALU.add))
    dve.need(t)
    t_start = dve.mark(V.tensor_scalar(start_i, c_c0, float(E), None, ALU.min))
    t = dve.mark(V.tensor_scalar(offs[:, 0, :], c_tile, float(C), None, ALU.mult))
    t_offs = dve.mark(V.tensor_scalar(offs[:, 1, :], c_tile, float(AW), None, ALU.mult))
    t_c = load_small(d_off.rearrange("o (g p) -> p o g", p=P), offs, t_offs)
    t_off = load_small(offr[0:1, :], d_off.rearrange("o (n u) -> u (o n)", u=1), t_c)

    lo = lo_E
    drow = view(lo, CG * CH, "p (g e) -> p g e", g=CG); lo += CG * CH
    irow = view(lo, CG * CH, "p (g e) -> p g e", g=CG); lo += CG * CH
    rel_bf = view(lo, CG * CH // 2, "p (g e) -> p g e", dt=bf16, g=CG); lo += CG * CH // 2
    ctile_p = tiny(CG)
    sort_edges(nc, d_dst, d_row, d_sorted, d_place, d_total, view(lo_sort, lo_E + E_SIZE - lo_sort), iota_row, iota_p,
               pool, unsorted, t_uns, tc_, *tw)
    s_win = [Slot(nc, f"win{i}") for i in range(2 * CG)]
    twin = []
    for g in range(CG):
        for q, (o, d) in enumerate(((drow, d_dst), (irow, d_row))):
            twin.append(s_win[2 * g + q].start(pool, lambda: G.indirect_dma_start(
                o[:, g, :], None, d[:, :], bass.IndirectOffsetOnAxis(ap=start_i[:, g:g + 1], axis=0)),
                t_start, tc_, *tw))
    dve.need(*twin)
    t = dve.mark(V.tensor_scalar(ctile_p, c_tile, float(P), None, ALU.mult))
    dve.need(t)
    for g in range(CG):
        t = dve.mark(V.tensor_scalar(drow[:, g, :], drow[:, g, :], ctile_p[:, g:g + 1], float(P), ALU.subtract, ALU.min))
    dve.need(t)
    t_rb = dve.mark(V.tensor_copy(rel_bf[:, :, :], drow[:, :, :]))
    t_rel = load_small(d_rel.rearrange("(g p) e -> p g e", p=P), rel_bf[:, :, :], t_rb)
    t = dve.mark(V.memset(flag[:, :, :], 0.0))
    dve.need(t)
    tmpf = view(lo, CG * CH, "p (g e) -> p g e", g=CG); lo += CG * CH
    t = dve.mark(V.tensor_tensor(out=tmpf[:, :, 1:CH], in0=drow[:, :, 1:CH], in1=drow[:, :, 0:CH - 1], op=ALU.not_equal))
    dve.need(t)
    t_flag = dve.mark(V.tensor_scalar(flag[:, :, 1:CH], tmpf[:, :, 1:CH], -BIG, None, ALU.mult))
    NQ = 4
    summ = tiny(NQ * CG * H).rearrange("p (q g h) -> p q g h", q=NQ, g=CG)
    unbroken = tiny(CG)
    t = dve.mark(V.tensor_reduce(unbroken, tmpf[:, :, 1:CH], AX.X, ALU.max))
    dve.need(t)
    t = dve.mark(V.tensor_scalar(unbroken, unbroken, -1.0, 1.0, ALU.mult, ALU.add))
    dve.need(t)
    for q, s_ in enumerate((drow[:, :, 0:1], drow[:, :, CH - 1:CH], c_tile.unsqueeze(2), unbroken.unsqueeze(2))):
        t_sum = dve.mark(V.tensor_copy(summ[:, q, :, :], s_.to_broadcast([P, CG, H])))
    pe.need(t_sum)
    for o, s_ in ((relE, drow), (idxE, irow)):
        for g in range(CG):
            k, bank = allb.take(pe)
            for j in range(HALF):
                ins = transpose(bank[:, j * P:(j + 1) * P], s_[:, g, j * P:(j + 1) * P])
            tp = pe.mark(ins)
            dve.need(tp)
            t_edge = allb.free[k] = dve.mark(V.tensor_copy(o[:, g, :, :], bank[:, 0:CH].rearrange("p (j c) -> p j c", j=HALF)))
    CR = [view(b_ + i * NCP, NCP)[0:H, :] for b_ in (lo_S + 3072, lo) for i in range(2)]
    lo += 2 * NCP
    assert lo <= lo_E + E_SIZE

    def to_rows(dst_row, src_pg, *tok):
        pe.need(*tok)
        k, bank = allb.take(pe)
        for g in range(CG):
            ins = transpose(bank[0:H, g * P:(g + 1) * P], src_pg(g))
        tp = pe.mark(ins)
        dve.need(tp)
        allb.free[k] = dve.mark(V.tensor_copy(dst_row, bank[0:H, :]))
        return allb.free[k]

    for q in range(NQ):
        t = to_rows(CR[q], lambda g: summ[:, q, g, :], t_sum)
    rF, rL, rT, rU = CR[0:4]
    eqp, brkA, brkB, eqn = (view(lo_cr + i * NCP // 2, NCP // 2, dt=bf16)[0:H, :] for i in range(4))
    dve.need(t)
    t = dve.mark(V.tensor_tensor(out=brkA[:, 1:], in0=rF[:, 1:], in1=rL[:, :NCP - 1], op=ALU.is_equal))
    t = dve.mark(V.tensor_tensor(out=brkB[:, 1:], in0=rT[:, 1:], in1=rT[:, :NCP - 1], op=ALU.is_equal))
    dve.need(t)
    t = dve.mark(V.memset(eqp[:, 0:1], 0.0))
    t = dve.mark(V.memset(eqn[:, NCP - 1:NCP], 0.0))
    t = dve.mark(V.tensor_tensor(out=eqp[:, 1:], in0=brkA[:, 1:], in1=brkB[:, 1:], op=ALU.mult))
    dve.need(t)
    t = dve.mark(V.tensor_copy(eqn[:, :NCP - 1], eqp[:, 1:]))
    dve.need(t)
    t = dve.mark(V.tensor_tensor(out=brkA, in0=eqp, in1=rU, op=ALU.mult))
    t = dve.mark(V.tensor_tensor(out=brkB, in0=eqn, in1=rU, op=ALU.mult))
    dve.need(t)
    for r_ in (brkA, brkB, eqp, eqn):
        t_cr = dve.mark(V.tensor_scalar(r_, r_, -1.0, BIG, ALU.add, ALU.mult))

    t_qz = dve.mark(V.memset(q_all[:, NT * C:(NT + 1) * C], 0.0))
    for _ in make_table(allb, d_ktab, t_Wk + t_Wq + [t_att], True, None, "both", False):
        pass
    k_done = list(tab_last)

    def background():
        tw_ = [load_small(Wt[:, t, :, :], vW[t].rearrange("(c p) n -> p c n", p=P), *k_done) for t in range(T)]
        tb_ = load_blocks(msg, *k_done)
        yield
        yield from make_table(bg, d_vtab, tw_ + tb_, False, None, "act", True)
        v_done.extend(tab_last)
        yield from mix()

    v_done = []
    mix_done = []

    def elu1(o, ps, tmp, tok, free):
        dve.need(tok, free)
        t = dve.mark(V.tensor_scalar(tmp, ps, 0.0, None, ALU.min))
        act.need(t)
        t = act.mark(A.activation(tmp, tmp, ACT.Exp))
        dve.need(t)
        return dve.mark(V.scalar_tensor_tensor(out=o, in0=ps, scalar=0.0, in1=tmp, op0=ALU.max, op1=ALU.add))

    def mix():
        lo = lo_B
        WKV = view(lo, CC * 2 * C, "p (c n) -> p c n", c=CC); lo += CC * 2 * C
        WQ = view(lo, CC * C, "p (c n) -> p c n", c=CC); lo += CC * C
        WM = view(lo, CC * C, "p (c n) -> p c n", c=CC); lo += CC * C
        W1 = view(lo, 4 * 512, "p (c n) -> p c n", c=4); lo += 4 * 512
        W2 = view(lo, 4 * C, "p (c n) -> p c n", c=4); lo += 4 * C
        g2row = view(lo, C); lo += C
        QT = view(lo, CC * 512, "p (c n) -> p c n", c=CC); lo += CC * 512
        KVB = view(lo, CC * P, "p (c n) -> p c n", c=CC); lo += CC * P
        KSB = view(lo, CC * P, "p (c n) -> p c n", c=CC); lo += CC * P
        bmask = view(lo, P); lo += P
        mT = view(lo, CC * 512, "p (c n) -> p c n", c=CC); lo += CC * 512
        lo_h = lo
        hT = view(lo, 4 * 512, "p (c n) -> p c n", c=4); lo += 4 * 512
        base = view(lo, GT * C, "p (t n) -> p t n", t=GT); lo += GT * C
        xh = view(lo, GT * C, "p (t n) -> p t n", t=GT); lo += GT * C
        assert lo <= lo_B + B_SIZE, (lo - lo_B, B_SIZE)
        Kb = [view(lo_h + i * C, C) for i in range(2)]
        Tb = [view(lo_h + 2 * C + i * C, C) for i in range(2)]
        VX = P + 1
        Vb = [view(lo_h + 4 * C + i * CC * VX, CC * VX, "p (c n) -> p c n", c=CC) for i in range(2)]
        tw_ = [load_small(WKV[:, :, 0:C], mWk.rearrange("(c p) n -> p c n", p=P), *v_done),
               load_small(WKV[:, :, C:2 * C], mWv.rearrange("(c p) n -> p c n", p=P), *v_done),
               load_small(WQ, mWq.rearrange("(c p) n -> p c n", p=P), *v_done),
               load_small(WM, mWm.rearrange("(c p) n -> p c n", p=P), *v_done),
               load_small(W1, mW1.rearrange("(c p) n -> p c n", p=P), *v_done),
               load_small(W2, mW2.rearrange("(c p) n -> p c n", p=P), *v_done),
               load_small(g2row, g2.rearrange("(o n) -> o n", o=1).to_broadcast([P, C]), *v_done),
               load_small(g1T, g1.rearrange("(c p) -> p c", p=P)),
               load_small(b1T, b1.rearrange("(c p) -> p c", p=P))]
        dve.need(*v_done)
        for i in range(2):
            for c in range(CC):
                t = dve.mark(V.memset(Vb[i][:, c, P:VX], 1.0))
        HM = 32
        t = dve.mark(V.memset(bmask, 0.0))
        dve.need(t)
        for b in range(P // HM):
            t_bm = dve.mark(V.memset(bmask[b * HM:(b + 1) * HM, b * HM:(b + 1) * HM], 1.0))
        yield
        k_free = [t_bm, t_bm]
        pe.need(*tw_)
        for tile in range(NT):
            rows = P if tile < NT - 1 else LAST
            i = tile % 2
            k, bank = bg.take(pe)
            for c in range(CC):
                ins = TE.matmul(bank[:, :], lhsT=xT[:, c, tile * P:(tile + 1) * P], rhs=WKV[:, c, :], start=c == 0, stop=c == CC - 1)
            tp = pe.mark(ins)
            act.need(tp, k_free[i])
            tv = act.mark(A.copy(Vb[i][:, :, 0:P], bank[:, C:2 * C].rearrange("p (c n) -> p c n", c=CC)))
            tk = elu1(Kb[i], bank[:, 0:C], Tb[i], tv, k_free[i])
            bg.free[k] = tk
            dve.need(tv)
            yield
            pe.need(tk, tv)
            for c in range(CC):
                ins = TE.matmul(banks[6 + c][:, 0:VX], lhsT=Kb[i][0:rows, c * P:(c + 1) * P], rhs=Vb[i][0:rows, c, :],
                                start=tile == 0, stop=tile == NT - 1)
            k_free[i] = tkv = pe.mark(ins)
            yield
        dve.need(tkv)
        for c in range(CC):
            t = dve.mark(V.scalar_tensor_tensor(out=KVB[:, c, :], in0=banks[6 + c][:, 0:P], scalar=1.0 / N, in1=bmask, op0=ALU.mult, op1=ALU.mult))
            t_kv = dve.mark(V.tensor_scalar(KSB[:, c, :], bmask, banks[6 + c][:, P:VX], None, ALU.mult))
        yield
        base_free = q_free = x_free_ = mT_free = h_free = tb_ = None
        s_b, s_bw = Slot(nc, "base_in"), Slot(nc, "base_out")
        h_free = tkv
        for g in range(NG):
            n = len(tiles_of(g))
            w = n * P
            cols = slice(g * 512, g * 512 + w)
            rows_d = d_base[g * 512:g * 512 + w, :].rearrange("(t p) n -> p t n", p=P)
            tb_ = s_b.start(sp, lambda: nc.sync.dma_start(base[:, 0:n, :], rows_d), base_free, *t_base_all)
            for c in range(CC):
                k, bank = bg.take(pe)
                for kc in range(CC):
                    ins = TE.matmul(bank[:, 0:w], lhsT=WQ[:, kc, c * P:(c + 1) * P], rhs=xT[:, kc, cols], start=kc == 0, stop=kc == CC - 1)
                tp = pe.mark(ins)
                tq = bg.free[k] = elu1(QT[:, c, 0:w], bank[:, 0:w], hT[:, c, 0:w], tp, h_free if c == 0 else None)
                yield
            pe.need(tq, t_kv)
            for c in range(CC):
                k, bank = bg.take(pe)
                tpn = pe.mark(TE.matmul(bank[:, 0:w], lhsT=KVB[:, c, :], rhs=QT[:, c, 0:w], start=True, stop=True))
                k2, bank2 = bg.take(pe)
                tpd = pe.mark(TE.matmul(bank2[:, 0:w], lhsT=KSB[:, c, :], rhs=QT[:, c, 0:w], start=True, stop=True))
                dve.need(tpd)
                t = bg.free[k2] = dve.mark(V.tensor_scalar(hT[:, 2 + c, 0:w], bank2[:, 0:w], ATT_EPS, None, ALU.add))
                dve.need(t)
                t = dve.mark(V.reciprocal(hT[:, 2 + c, 0:w], hT[:, 2 + c, 0:w]))
                dve.need(t, tpn, tpd)
                tm = bg.free[k] = dve.mark(V.scalar_tensor_tensor(out=hT[:, c, 0:w], in0=bank[:, 0:w], scalar=float(N), in1=hT[:, 2 + c, 0:w], op0=ALU.mult, op1=ALU.mult))
                yield
            pe.need(tm)
            kb, tps = [], []
            for i0 in range(0, n, 2):
                k, bank = bg.take(pe)
                for i4 in range(i0, min(n, i0 + 2)):
                    for c in range(CC):
                        ins = TE.matmul(bank[:, (i4 - i0) * C:(i4 - i0 + 1) * C], lhsT=hT[:, c, i4 * P:(i4 + 1) * P], rhs=WM[:, c, :],
                                        start=c == 0, stop=c == CC - 1)
                tps.append(pe.mark(ins))
                kb += [(k, bank, j) for j in range(min(n, i0 + 2) - i0)]
                yield
            h_free = tps[-1]
            t = ln_stats([b_[:, j * C:(j + 1) * C] for _, b_, j in kb], tps[-1])
            dve.need(t, x_free_)
            for i4, (k, bank, j) in enumerate(kb):
                t = bg.free[k] = dve.mark(V.tensor_scalar(xh[:, i4, :], bank[:, j * C:(j + 1) * C], mv[:, i4, 0:1], rstd[:, i4:i4 + 1], ALU.subtract, ALU.mult))
            yield
            pe.need(t)
            for c in range(CC):
                k, bank = bg.take(pe)
                for i4 in range(n):
                    ins = transpose(bank[:, i4 * P:(i4 + 1) * P], xh[:, i4, c * P:(c + 1) * P])
                x_free_ = tp = pe.mark(ins)
                act.need(tp, mT_free, *tw_)
                tmt = bg.free[k] = act.mark(A.activation(mT[:, c, 0:w], bank[:, 0:w], ACT.Identity, bias=b1T[:, c:c + 1], scale=g1T[:, c:c + 1]))
            yield
            pe.need(tmt)
            for oc in range(4):
                k, bank = bg.take(pe)
                for kc in range(4):
                    rhs = xT[:, kc, cols] if kc < CC else mT[:, kc - CC, 0:w]
                    ins = TE.matmul(bank[:, 0:w], lhsT=W1[:, kc, oc * P:(oc + 1) * P], rhs=rhs, start=kc == 0, stop=kc == 3)
                tp = pe.mark(ins)
                act.need(tp, h_free)
                th = bg.free[k] = act.mark(A.activation(hT[:, oc, 0:w], bank[:, 0:w], ACT.Relu))
                yield
            mT_free = tp
            pe.need(th)
            kb = []
            for i0 in range(0, n, 2):
                k, bank = bg.take(pe)
                for i4 in range(i0, min(n, i0 + 2)):
                    for kc in range(4):
                        ins = TE.matmul(bank[:, (i4 - i0) * C:(i4 - i0 + 1) * C], lhsT=hT[:, kc, i4 * P:(i4 + 1) * P], rhs=W2[:, kc, :],
                                        start=kc == 0, stop=kc == 3)
                tp = pe.mark(ins)
                kb += [(k, bank, j) for j in range(min(n, i0 + 2) - i0)]
                yield
            h_free = tp
            t = ln_stats([b_[:, j * C:(j + 1) * C] for _, b_, j in kb], tp)
            dve.need(t, tb_, x_free_, *tw_)
            for i4, (k, bank, j) in enumerate(kb):
                t = bg.free[k] = dve.mark(V.scalar_tensor_tensor(out=xh[:, i4, :], in0=bank[:, j * C:(j + 1) * C], scalar=mv[:, i4, 0:1],
                                                                in1=g2row, op0=ALU.subtract, op1=ALU.mult))
            dve.need(t)
            for i4 in range(n):
                t = dve.mark(V.scalar_tensor_tensor(out=base[:, i4, :], in0=xh[:, i4, :], scalar=rstd[:, i4:i4 + 1],
                                                    in1=base[:, i4, :], op0=ALU.mult, op1=ALU.add))
            x_free_ = t
            base_free = s_bw.start(sp, lambda: nc.sync.dma_start(rows_d, base[:, 0:n, :]), t)
            yield
        mix_done.extend([base_free, h_free, x_free_, mT_free, th, tmt])

    lo = lo_E
    NR = 5
    ring = [view(lo + i * HALF * C, HALF * C, "p (j n) -> p j n", j=HALF) for i in range(NR)]; lo += NR * HALF * C
    lo_E2 = lo
    RB = 4
    relB = [view(lo + i * RB * CH // 2, RB * CH // 2, "p (k e) -> p k e", dt=bf16, k=RB) for i in range(2)]; lo += RB * CH
    oh = [view(lo + i * CH, CH) for i in range(3)]; lo += 3 * CH
    prod = [view(lo + i * HALF * C, HALF * C) for i in range(1)]; lo += HALF * C
    assert lo <= lo_E + E_SIZE
    s_ring = [[Slot(nc, f"gather{i}_{j}") for j in range(HALF)] for i in range(NR)]
    s_relB = [Slot(nc, f"relB{i}") for i in range(2)]
    ring_free = [None] * NR
    tabtok = []
    got = {}

    def gather(i, table):
        g, c = divmod(i, P)
        s = i % NR
        toks = []
        for j in range(HALF):
            toks.append(s_ring[s][j].start(pool, lambda: G.indirect_dma_start(
                ring[s][:, j, :], None, table[:, :], bass.IndirectOffsetOnAxis(ap=idxE[:, g, j, c:c + 1], axis=0)),
                t_edge, t_cr, ring_free[s], *tabtok))
        got[i] = toks

    work = background()
    spent = [0]

    def advance(n):
        for _ in range(n):
            next(work, None)

    tabtok[:] = k_done
    LOOK = NR - 1
    relB_free = [None, None]
    t_relB = [None, None]

    def load_relB(kb):
        s = kb % 2
        n = min(RB, NCH - kb * RB)
        t_relB[s] = s_relB[s].start(sp, lambda: nc.sync.dma_start(
            relB[s][:, 0:n, :], d_rel[kb * RB:kb * RB + n, :].rearrange("(o k) e -> o (k e)", o=1).to_broadcast([P, n * CH])),
            t_rel, t_edge, t_cr, relB_free[s])

    load_relB(0)
    load_relB(1)
    for i in range(min(LOOK, NCH)):
        gather(i, d_ktab)
    oh_free, prod_free = [t_cr] * 3, [t_cr] * 2
    t_oh = {}
    reg_batch = {}

    def offsets(i, row, eng, limit):
        if i % 8 == 0:
            n = min(8, NCP - i)
            _, vals = nc.values_load_multi_w_load_instructions(
                offr[0:1, row * NCP + i:row * NCP + i + n], engines=[eng], min_val=0, max_val=limit,
                skip_runtime_bounds_check_because="a chunk's tile is at most the number of tiles")
            reg_batch[eng] = vals
        return reg_batch[eng][i % 8]

    def make_oh(i):
        s, b = i % 3, (i // RB) % 2
        dve.need(t_relB[b], oh_free[s])
        t_oh[i] = dve.mark(V.tensor_scalar(oh[s], relB[b][:, i % RB, :], iota_p, None, ALU.is_equal))
        if i % RB == RB - 1 or i == NCH - 1:
            relB_free[b] = t_oh[i]
            if (i // RB + 2) * RB < NCH:
                load_relB(i // RB + 2)

    make_oh(0)
    make_oh(1)
    pe.need(t_off, t_qz, *k_done)
    STEPS1 = 1
    t_sc = t_cr
    for i in range(NCH):
        g, c = divmod(i, P)
        if i + LOOK < NCH:
            gather(i + LOOK, d_ktab)
        k, bank = fg.take(pe)
        off = offsets(i, 0, mybir.EngineType.PE, NT * C)
        pe.need(t_oh[i])
        for j in range(HALF):
            ins = TE.matmul(bank[:, j * C:(j + 1) * C], lhsT=oh[i % 3][:, j * P:(j + 1) * P],
                            rhs=q_all[:, bass.ds(off, C)], start=True, stop=True)
        oh_free[i % 3] = tp = pe.mark(ins)
        if i + 2 < NCH:
            make_oh(i + 2)
        pr_ = prod[0]
        dve.need(tp, *got[i], t_sc)
        t = fg.free[k] = ring_free[i % NR] = dve.mark(V.tensor_tensor(out=pr_, in0=bank[:, :], in1=ring[i % NR].rearrange("p j n -> p (j n)"), op=ALU.mult))
        dve.need(t)
        t_sc = dve.mark(V.tensor_reduce(S_all[:, :, g, :, c].rearrange("p h j -> p j h"),
                                        pr_.rearrange("p (j h d) -> p j h d", j=HALF, h=H), AX.X, ALU.add))
        advance(STEPS1)

    while not v_done:
        advance(1)
    tabtok[:] = v_done
    for i in range(LOOK):
        gather(i, d_vtab)

    lastc = NCH - (CG - 1) * P
    tz = dve.mark(V.memset(S_all[:, :, CG - 1, :, lastc:P], 0.0))
    lo = lo_E2
    F = [view(lo + i * CH, CH) for i in range(4)]; lo += 4 * CH
    LM = view(lo, CG * H, "p (g h) -> p g h", g=CG); lo += CG * H
    FM = view(lo, CG * H, "p (g h) -> p g h", g=CG); lo += CG * H
    cF = view(lo, CG * H, "p (g h) -> p g h", g=CG); lo += CG * H
    cB = view(lo, CG * H, "p (g h) -> p g h", g=CG); lo += CG * H
    pe.need(t_sc, tz)
    for h in range(H):
        for g in range(CG):
            k, bank = fg.take(pe)
            for j in range(HALF):
                ins = transpose(bank[:, j * P:(j + 1) * P], S_all[:, h, g, j, :])
            tp = pe.mark(ins)
            act.need(tp)
            t_tr = fg.free[k] = act.mark(A.copy(S_row[:, h, g, :], bank[:, 0:CH]))
    dve.need(t_tr, tp)
    n_ = 0
    ff = [None] * 4
    for h in range(H):
        for g in range(CG):
            a, b = F[2 * (n_ % 2)], F[2 * (n_ % 2) + 1]
            t = dve.mark(V.tensor_tensor_scan(out=a, data0=flag[:, g, 0:CH], data1=S_row[:, h, g, :], initial=-BIG, op0=ALU.add, op1=ALU.max))
            dve.need(t)
            t = dve.mark(V.tensor_copy(LM[:, g, h:h + 1], a[:, CH - 1:CH]))
            t = dve.mark(V.tensor_tensor_scan(out=b[:, ::-1], data0=flag[:, g, 1:CH + 1][:, ::-1], data1=a[:, ::-1], initial=-BIG, op0=ALU.add, op1=ALU.max))
            dve.need(t)
            t = dve.mark(V.tensor_copy(FM[:, g, h:h + 1], b[:, 0:1]))
            n_ += 1
    rFM, rLM, rCF, rCB = (view(lo_big + i * NCP, NCP)[0:H, :] for i in range(4))
    allb = Banks(banks[0:2])
    allb.free = list(fg.free[0:2])
    t1 = to_rows(rLM, lambda g: LM[:, g, :], t)
    t2 = to_rows(rFM, lambda g: FM[:, g, :], t)
    dve.need(t1, t2)
    t = dve.mark(V.tensor_tensor_scan(out=rLM, data0=brkA, data1=rLM, initial=-BIG, op0=ALU.add, op1=ALU.max))
    t = dve.mark(V.tensor_tensor_scan(out=rFM[:, ::-1], data0=brkB[:, ::-1], data1=rFM[:, ::-1], initial=-BIG, op0=ALU.add, op1=ALU.max))
    dve.need(t)
    t = dve.mark(V.memset(rCF[:, 0:1], -BIG))
    t = dve.mark(V.memset(rCB[:, NCP - 1:NCP], -BIG))
    t = dve.mark(V.tensor_tensor(out=rCF[:, 1:], in0=rLM[:, :NCP - 1], in1=eqp[:, 1:], op=ALU.add))
    t = dve.mark(V.tensor_tensor(out=rCB[:, :NCP - 1], in0=rFM[:, 1:], in1=eqn[:, :NCP - 1], op=ALU.add))
    pe.need(t)
    for o, r_ in ((cF, rCF), (cB, rCB)):
        k, bank = allb.take(pe)
        for g in range(CG):
            ins = TE.transpose(bank[:, g * H:(g + 1) * H], r_[:, g * P:(g + 1) * P], ident[0:H, 0:H])
        tp = pe.mark(ins)
        dve.need(tp)
        t = allb.free[k] = dve.mark(V.tensor_copy(o[:, :, :], bank[:, 0:CG * H].rearrange("p (g h) -> p g h", g=CG)))
    fg.free[0:2] = allb.free
    dve.need(t)
    n_ = 0
    for h in range(H):
        for g in range(CG):
            a, b = F[2 * (n_ % 2)], F[2 * (n_ % 2) + 1]
            t = dve.mark(V.tensor_tensor_scan(out=a, data0=flag[:, g, 0:CH], data1=S_row[:, h, g, :], initial=cF[:, g, h:h + 1], op0=ALU.add, op1=ALU.max))
            dve.need(t)
            t = dve.mark(V.tensor_tensor_scan(out=b[:, ::-1], data0=flag[:, g, 1:CH + 1][:, ::-1], data1=a[:, ::-1], initial=cB[:, g, h:h + 1], op0=ALU.add, op1=ALU.max))
            dve.need(t)
            t = dve.mark(V.tensor_tensor(out=S_row[:, h, g, :], in0=S_row[:, h, g, :], in1=b, op=ALU.subtract))
            act.need(t)
            tx_ = act.mark(A.activation(S_row[:, h, g, :], S_row[:, h, g, :], ACT.Exp))
            pe.need(tx_)
            k, bank = fg.take(pe)
            for j in range(HALF):
                ins = transpose(bank[:, j * P:(j + 1) * P], S_row[:, h, g, j * P:(j + 1) * P])
            tp = pe.mark(ins)
            act.need(tp)
            t_ex = fg.free[k] = act.mark(A.copy(S_all[:, h, g, :, :], bank[:, 0:CH].rearrange("p (j c) -> p j c", j=HALF)))
            n_ += 1

    lo = lo_E2
    so = [view(lo + i * HALF * P, HALF * P) for i in range(3)]; lo += 3 * HALF * P
    Rv = [view(lo + i * HALF * AW, HALF * AW, "p (j n) -> p j n", j=HALF) for i in range(3)]; lo += 3 * HALF * AW
    assert lo <= lo_E + E_SIZE
    t_z = dve.mark(V.memset(acc, 0.0))
    dve.need(t_ex, t_z, t_off)
    so_free, r_free = [None] * 3, [None] * 3
    t_acc = t_z
    pend = []
    STEPS2 = 1

    def finish_chunk(i, k, bank, tp):
        nonlocal t_acc
        off = offsets(i, 1, mybir.EngineType.DVE, NT * AW)
        dve.need(tp, t_acc)
        t_acc = fg.free[k] = dve.mark(V.tensor_tensor(out=acc[:, bass.ds(off, AW)], in0=acc[:, bass.ds(off, AW)], in1=bank[:, 0:AW], op=ALU.add))

    for i in range(NCH):
        g, c = divmod(i, P)
        if i + LOOK < NCH:
            gather(i + LOOK, d_vtab)
        s = i % 3
        dve.need(so_free[s])
        for j in range(HALF):
            t_so = dve.mark(V.tensor_scalar(so[s][:, j * P:(j + 1) * P], iota_row, relE[:, g, j, c:c + 1], None, ALU.is_equal))
        ex = S_all[:, :, g, :, c].rearrange("p h j -> p j h")
        dve.need(*got[i])
        for j in range(HALF):
            t_r = ring_free[i % NR] = dve.mark(V.tensor_tensor(
                out=Rv[s][:, j, 0:C].rearrange("p (h d) -> p h d", h=H), in0=ring[i % NR][:, j, :].rearrange("p (h d) -> p h d", h=H),
                in1=ex[:, j, :].unsqueeze(2).to_broadcast([P, H, DK]), op=ALU.mult))
        act.need(r_free[s], t_ex, t_z)
        t_a = act.mark(A.copy(Rv[s][:, :, C:AW], ex))
        pe.need(t_r, t_a, t_so)
        k, bank = fg.take(pe)
        for j in range(HALF):
            ins = TE.matmul(bank[:, 0:AW], lhsT=so[s][:, j * P:(j + 1) * P], rhs=Rv[s][:, j, :], start=j == 0, stop=j == HALF - 1)
        so_free[s] = r_free[s] = tp = pe.mark(ins)
        pend.append((i, k, bank, tp))
        if len(pend) > 1:
            finish_chunk(*pend.pop(0))
        advance(STEPS2)
    finish_chunk(*pend.pop(0))
    for _ in work:
        pass

    ALLB = Banks(banks)
    ALLB.free = [t_acc] * 8
    pe.need(t_acc, *mix_done)
    done = [t_acc, tp, t_a] + mix_done
    lo = lo_B
    Wa = view(lo, T * CC * C, "p (t c n) -> p t c n", t=T, c=CC); lo += T * CC * C
    F1 = view(lo, CC * FF, "p (c n) -> p c n", c=CC); lo += CC * FF
    F2 = view(lo, FC * C, "p (c n) -> p c n", c=FC); lo += FC * C
    hF = view(lo, FC * 512, "p (c n) -> p c n", c=FC); lo += FC * 512
    fb2row = view(lo, C); lo += C
    assert lo <= lo_B + B_SIZE
    ta_ = [load_small(Wa[:, t, :, :], aW[t].rearrange("(c p) n -> p c n", p=P), *done) for t in range(T)]
    tf_ = [load_small(F1, fw1.rearrange("(c p) n -> p c n", p=P), *done),
           load_small(F2, fw2.rearrange("(c p) n -> p c n", p=P), *done),
           load_small(fb2row, fb2.rearrange("(o n) -> o n", o=1).to_broadcast([P, C]), *done),
           load_small(fb1T, fb1.rearrange("(c p) -> p c", p=P)),
           load_small(brP, br.rearrange("(o n) -> o n", o=1).to_broadcast([P, 1])),
           load_small(wrT, wr.rearrange("(c p) o -> p (c o)", p=P)),
           load_small(skipP, skip.rearrange("(o n) -> o n", o=1).to_broadcast([P, T]))]
    lo = lo_S
    ntT = view(lo, NT, dt=i32); lo += NT
    skn = view(lo, NT); lo += NT
    wS = view(lo, NT); lo += NT
    wsel = view(lo, NT); lo += NT
    key, khi, klo, eqm, cum, colt = (view(lo + i * NT, NT) for i in range(6)); lo += 6 * NT
    lo_S2 = lo
    tn0 = dve.mark(V.memset(ntT, 0))
    tn_ = [load_small(ntT[:, 0:NT - 1], ntype[0:(NT - 1) * P].rearrange("(t p) -> p t", p=P), tn0, t_acc, t_a, tp),
           load_small(ntT[0:LAST, NT - 1:NT], ntype[(NT - 1) * P:N].rearrange("(p o) -> p o", o=1), tn0, t_acc, t_a, tp)]
    act.need(*tf_)
    t = act.mark(A.activation(skipP, skipP, ACT.Exp, scale=-1.0))
    dve.need(t)
    t = dve.mark(V.tensor_scalar(skipP, skipP, 1.0, None, ALU.add))
    dve.need(t)
    t = dve.mark(V.reciprocal(skipP, skipP))
    dve.need(t, *tn_)
    t = dve.mark(V.tensor_scalar(skn, ntT, 0.0, skipP[:, 0:1], ALU.is_equal, ALU.mult))
    for ty in range(1, T):
        dve.need(t)
        t = dve.mark(V.tensor_scalar(cum, ntT, float(ty), skipP[:, ty:ty + 1], ALU.is_equal, ALU.mult))
        dve.need(t)
        t = dve.mark(V.tensor_tensor(out=skn, in0=skn, in1=cum, op=ALU.add))
    t_skn = t

    lo = lo_E
    ag = view(lo, GT * C, "p (t n) -> p t n", t=GT); lo += GT * C
    x1 = [view(lo + i * GT * C, GT * C, "p (t n) -> p t n", t=GT) for i in range(2)]; lo += 2 * GT * C
    MA = view(lo, CC * T * P, "p (t c n) -> p t c n", t=T, c=CC); lo += CC * T * P
    aT = view(lo, CC * P, "p (c n) -> p c n", c=CC); lo += CC * P
    rden = view(lo, GT * H, "p (t h) -> p t h", t=GT); lo += GT * H
    ntr2 = [view(lo + i * 512, 512, dt=i32) for i in range(2)]; lo += 1024
    assert lo <= lo_E + E_SIZE, lo - lo_E
    s_b2 = [Slot(nc, f"x1in{i}") for i in range(2)]
    s_b3 = [Slot(nc, f"x1out{i}") for i in range(2)]
    s_nt2 = [Slot(nc, f"nt2_{i}") for i in range(2)]
    x1_free, nt_free = list([t_acc] * 2), [t_acc] * 2
    ag_free = ma_free = None
    accv = acc.rearrange("p (t n) -> p t n", n=AW)
    dve.need(*done)
    x1T_ready = None
    d_out = []
    for g in range(NG):
        ts = tiles_of(g)
        n = len(ts)
        w = n * P
        s = g % 2
        valid = min(N - g * 512, w)
        rows_d = d_base[g * 512:g * 512 + w, :].rearrange("(t p) n -> p t n", p=P)
        tb_ = s_b2[s].start(sp, lambda: nc.sync.dma_start(x1[s][:, 0:n, :], rows_d), x1_free[s], *done)
        tn = s_nt2[s].start(sp, lambda: nc.sync.dma_start(
            ntr2[s][:, 0:valid], ntype[g * 512:g * 512 + valid].rearrange("(o n) -> o n", o=1).to_broadcast([P, valid])), nt_free[s], *done)
        if valid < w:
            dve.need(nt_free[s])
            tm = dve.mark(V.memset(ntr2[s][:, valid:w], 0))
            dve.need(tm)
        t = dve.mark(V.tensor_scalar(rden[:, 0:n, :], accv[:, ts[0]:ts[0] + n, C:AW], 0.5, None, ALU.max))
        dve.need(t)
        t = dve.mark(V.reciprocal(rden[:, 0:n, :], rden[:, 0:n, :]))
        dve.need(t, ag_free)
        for i4 in range(n):
            t = dve.mark(V.tensor_tensor(out=ag[:, i4, :].rearrange("p (h d) -> p h d", h=H),
                                         in0=accv[:, ts[i4], 0:C].rearrange("p (h d) -> p h d", h=H),
                                         in1=rden[:, i4, :].unsqueeze(2).to_broadcast([P, H, DK]), op=ALU.mult))
        pe.need(t)
        for i4 in range(n):
            k, bank = ALLB.take(pe)
            for c in range(CC):
                ins = transpose(bank[:, c * P:(c + 1) * P], ag[:, i4, c * P:(c + 1) * P])
            tp = pe.mark(ins)
            act.need(tp, ma_free)
            ta2 = ALLB.free[k] = act.mark(A.copy(aT[:, :, :], bank[:, 0:C].rearrange("p (c n) -> p c n", c=CC)))
            dve.need(ta2, tn, ma_free)
            for ty in range(T):
                tm = dve.mark(V.scalar_tensor_tensor(
                    out=MA[:, ty, :, :], in0=ntr2[s][:, i4 * P:(i4 + 1) * P].unsqueeze(1).to_broadcast([P, CC, P]), scalar=float(ty),
                    in1=aT[:, :, :], op0=ALU.is_equal, op1=ALU.mult))
            pe.need(tm, *ta_)
            k, bank = ALLB.take(pe)
            for i in range(T * CC):
                ty, c = divmod(i, CC)
                ins = TE.matmul(bank[:, 0:C], lhsT=MA[:, ty, c, :], rhs=Wa[:, ty, c, :], start=i == 0, stop=i == T * CC - 1)
            ma_free = tp = pe.mark(ins)
            dve.need(tp, tb_, t_skn)
            t = ALLB.free[k] = dve.mark(V.scalar_tensor_tensor(out=x1[s][:, i4, :], in0=bank[:, 0:C], scalar=skn[:, ts[i4]:ts[i4] + 1],
                                                              in1=x1[s][:, i4, :], op0=ALU.mult, op1=ALU.add))
        ag_free = tp
        nt_free[s] = tm
        t = ln_stats([x1[s][:, i, :] for i in range(n)], t)
        dve.need(t, ag_free)
        for i4 in range(n):
            t = dve.mark(V.tensor_scalar(ag[:, i4, :], x1[s][:, i4, :], mv[:, i4, 0:1], rstd[:, i4:i4 + 1], ALU.subtract, ALU.mult))
        dve.need(t)
        t_xl = t
        t = dve.mark(V.tensor_tensor(out=x1[s][:, 0:n, :], in0=x1[s][:, 0:n, :], in1=ag[:, 0:n, :], op=ALU.add))
        x1_free[s] = s_b3[s].start(sp, lambda: nc.sync.dma_start(rows_d, x1[s][:, 0:n, :]), t)
        pe.need(t_xl)
        for c in range(CC):
            k, bank = ALLB.take(pe)
            for i4 in range(n):
                ins = transpose(bank[:, i4 * P:(i4 + 1) * P], ag[:, i4, c * P:(c + 1) * P])
            tp = pe.mark(ins)
            act.need(tp)
            tt = ALLB.free[k] = act.mark(A.copy(xT[:, c, g * 512:g * 512 + w], bank[:, 0:w]))
        ag_free = tp
        pe.need(tt, *tf_)
        k, bank = ALLB.take(pe)
        for i4 in range(n):
            for c in range(CC):
                ins = TE.matmul(bank[:, i4:i4 + 1], lhsT=xT[:, c, g * 512 + i4 * P:g * 512 + (i4 + 1) * P], rhs=wrT[:, c:c + 1],
                                start=c == 0, stop=c == CC - 1)
        tp = pe.mark(ins)
        dve.need(tp, *tf_)
        t_w = ALLB.free[k] = dve.mark(V.tensor_scalar(wS[:, ts[0]:ts[0] + n], bank[:, 0:n], brP, None, ALU.add))
    x1_all = list(x1_free)

    dve.need(t_w)
    ki, hi_i, lo_i = key.bitcast(i32), khi.bitcast(i32), klo.bitcast(i32)
    t = dve.mark(V.tensor_scalar(ki, wS.bitcast(i32), 31, -2147483648, ALU.arith_shift_right, ALU.bitwise_or))
    dve.need(t)
    t = dve.mark(V.tensor_tensor(out=ki, in0=ki, in1=wS.bitcast(i32), op=ALU.bitwise_xor))
    dve.need(t)
    t = dve.mark(V.tensor_scalar(hi_i, ki, 16, None, ALU.logical_shift_right))
    t = dve.mark(V.tensor_scalar(lo_i, ki, 65535, None, ALU.bitwise_and))
    dve.need(t)
    t = dve.mark(V.tensor_copy(khi, hi_i))
    t = dve.mark(V.tensor_copy(klo, lo_i))
    dve.need(t)
    lo = lo_S2
    padm = view(lo, 1); lo += 1
    cntp, tot, thr, step_, cand, keep = (view(lo + i, 1) for i in range(6)); lo += 6
    cmpv = view(lo, NT); lo += NT
    tri = view(lo, P); lo += P
    selv = view(lo, NT); lo += NT
    t = dve.mark(V.tensor_scalar(padm, iota_p, float(LAST), None, ALU.is_lt))
    dve.need(t)
    for q in (khi, klo):
        t = dve.mark(V.tensor_scalar(q[:, NT - 1:NT], q[:, NT - 1:NT], 1.0, padm, ALU.add, ALU.mult))
        dve.need(t)
        t = dve.mark(V.tensor_scalar(q[:, NT - 1:NT], q[:, NT - 1:NT], 1.0, None, ALU.subtract))
        dve.need(t)

    def count(src, thr_ap, op, tok):
        dve.need(tok)
        t = dve.mark(V.tensor_scalar(cmpv, src, thr_ap, None, op, ALU.add, accum_out=cntp))
        pe.need(t)
        k, bank = ALLB.take(pe)
        tp = pe.mark(TE.matmul(bank[:, 0:1], lhsT=ones, rhs=cntp, start=True, stop=True))
        dve.need(tp)
        return k, bank

    def largest(src, tok):
        dve.need(tok)
        t = dve.mark(V.memset(thr, 0.0))
        for bit in range(15, -1, -1):
            dve.need(t)
            t = dve.mark(V.tensor_scalar(cand, thr, float(1 << bit), None, ALU.add))
            k, bank = count(src, cand, ALU.is_ge, t)
            t = ALLB.free[k] = dve.mark(V.tensor_scalar(keep, bank[:, 0:1], float(KK), float(1 << bit), ALU.is_ge, ALU.mult))
            dve.need(t)
            t = dve.mark(V.tensor_tensor(out=thr, in0=thr, in1=keep, op=ALU.add))
        return t

    t = largest(khi, t)
    dve.need(t)
    t = dve.mark(V.tensor_scalar(eqm, khi, thr, None, ALU.is_equal))
    dve.need(t)
    t = dve.mark(V.scalar_tensor_tensor(out=klo, in0=klo, scalar=1.0, in1=eqm, op0=ALU.add, op1=ALU.mult))
    t = dve.mark(V.tensor_scalar(cum, khi, thr, 65537.0, ALU.is_gt, ALU.mult))
    dve.need(t)
    t = dve.mark(V.tensor_tensor(out=klo, in0=klo, in1=cum, op=ALU.add))
    dve.need(t)
    t = dve.mark(V.tensor_scalar(klo, klo, -1.0, None, ALU.add))
    t = largest(klo, t)
    k, bank = count(klo, thr, ALU.is_gt, t)
    need_ = tot
    t = ALLB.free[k] = dve.mark(V.tensor_scalar(need_, bank[:, 0:1], -1.0, float(KK), ALU.mult, ALU.add))
    t = dve.mark(V.tensor_scalar(selv, klo, thr, None, ALU.is_gt))
    t = dve.mark(V.tensor_scalar(eqm, klo, thr, None, ALU.is_equal))
    t_tri = dve.mark(V.tensor_scalar(tri, iota_row, iota_p, None, ALU.is_gt))
    pe.need(t, t_tri)
    k, bank = ALLB.take(pe)
    TE.matmul(bank[:, 0:NT], lhsT=tri, rhs=eqm, start=True, stop=True)
    tp = pe.mark(TE.matmul(bank[:, 64:64 + NT], lhsT=ones, rhs=eqm, start=True, stop=True))
    dve.need(tp, t_tri)
    t = dve.mark(V.tensor_copy(colt, bank[:, 64:64 + NT]))
    dve.need(t)
    t = dve.mark(V.memset(cum[:, 0:1], 0.0))
    t = dve.mark(V.tensor_tensor_scan(out=cum[:, 1:NT], data0=colt[:, 0:NT - 1], data1=colt[:, 0:NT - 1], initial=0.0, op0=ALU.add, op1=ALU.bypass))
    dve.need(t)
    t = ALLB.free[k] = dve.mark(V.tensor_tensor(out=cum, in0=cum, in1=bank[:, 0:NT], op=ALU.add))
    dve.need(t)
    t = dve.mark(V.scalar_tensor_tensor(out=eqm, in0=cum, scalar=need_, in1=eqm, op0=ALU.is_lt, op1=ALU.mult))
    dve.need(t)
    t = dve.mark(V.tensor_tensor(out=selv, in0=selv, in1=eqm, op=ALU.add))
    dve.need(t)
    t_sel = dve.mark(V.tensor_tensor(out=wsel, in0=wS, in1=selv, op=ALU.mult))

    s_o = [Slot(nc, f"out{i}") for i in range(2)]
    lo = lo_E
    yb = [view(lo + i * GT * C, GT * C, "p (t n) -> p t n", t=GT) for i in range(2)]; lo += 2 * GT * C
    xb2 = [view(lo + i * GT * C, GT * C, "p (t n) -> p t n", t=GT) for i in range(2)]; lo += 2 * GT * C
    x2_free, h_free = [None, None], None
    sp.need(*x1_all, t_w)
    dve.need(*x1_all)
    s_b4 = [Slot(nc, f"x2in{i}") for i in range(2)]
    for g in range(NG):
        ts = tiles_of(g)
        n = len(ts)
        w = n * P
        s = g % 2
        rows_d = d_base[g * 512:g * 512 + w, :].rearrange("(t p) n -> p t n", p=P)
        tb_ = s_b4[s].start(sp, lambda: nc.sync.dma_start(xb2[s][:, 0:n, :], rows_d), x2_free[s], *x1_all, ag_free, tp)
        for oc in range(FC):
            k, bank = ALLB.take(pe)
            for c in range(CC):
                ins = TE.matmul(bank[:, 0:w], lhsT=F1[:, c, oc * P:(oc + 1) * P], rhs=xT[:, c, g * 512:g * 512 + w], start=c == 0, stop=c == CC - 1)
            tp = pe.mark(ins)
            act.need(tp, h_free)
            th = ALLB.free[k] = act.mark(A.activation(hF[:, oc, 0:w], bank[:, 0:w], ACT.Gelu_apprx_tanh, bias=fb1T[:, oc:oc + 1]))
        pe.need(th)
        for i4 in range(n):
            k, bank = ALLB.take(pe)
            for c in range(FC):
                ins = TE.matmul(bank[:, 0:C], lhsT=hF[:, c, i4 * P:(i4 + 1) * P], rhs=F2[:, c, :], start=c == 0, stop=c == FC - 1)
            tp = pe.mark(ins)
            dve.need(tp, t_sel, x2_free[s], tb_)
            t = ALLB.free[k] = dve.mark(V.tensor_tensor(out=yb[s][:, i4, :], in0=bank[:, 0:C], in1=fb2row, op=ALU.add))
            dve.need(t)
            t = dve.mark(V.scalar_tensor_tensor(out=yb[s][:, i4, :], in0=yb[s][:, i4, :], scalar=wsel[:, ts[i4]:ts[i4] + 1],
                                                in1=xb2[s][:, i4, :], op0=ALU.mult, op1=ALU.add))
        h_free = tp
        if g < NG - 1:
            x2_free[s] = s_o[s].start(sp, lambda: nc.sync.dma_start(out[g * 512:g * 512 + w, :].rearrange("(t p) n -> p t n", p=P), yb[s][:, 0:n, :]), t)
        else:
            x2_free[s] = s_o[s].start(sp, lambda: nc.sync.dma_start(out[g * 512:N, :], yb[s][0:LAST, 0, :]), t)
    sp.need(s_o[0].last, s_o[1].last)


_INS = ["x", "src", "dst", "edge_type_8", "node_type_4", "L0_gnn_k_linears", "L0_gnn_q_linears", "L0_gnn_v_linears",
        "L0_gnn_a_linears", "L0_gnn_relation_att", "L0_gnn_relation_msg", "L0_gnn_relation_pri", "L0_gnn_skip",
        "L0_mix_Wq", "L0_mix_Wk", "L0_mix_Wv", "L0_mix_Wm", "L0_mix_W1", "L0_mix_W2", "L0_mix_g1", "L0_mix_b1",
        "L0_mix_g2", "L0_mix_b2", "L0_ffn_wr", "L0_ffn_br", "L0_ffn_w1", "L0_ffn_b1", "L0_ffn_w2", "L0_ffn_b2"]


def kernel(**inputs):
    import numpy as _np
    import concourse.bacc as _bacc
    from concourse.bass_utils import run_bass_kernel_spmd as _run

    nc = _bacc.Bacc("TRN2", target_bir_lowering=False, num_devices=1)
    arrays, args = {}, []
    for name in _INS:
        a = _np.ascontiguousarray(inputs[name])
        arrays["in_" + name] = a
        args.append(nc.dram_tensor("in_" + name, a.shape, mybir.dt.from_np(a.dtype), kind="ExternalInput").ap())
    o = nc.dram_tensor("out_x", (N, C), f32, kind="ExternalOutput").ap()
    build(nc, *args, o)
    r = _run(nc, [arrays], core_ids=[0])
    return r.results[0]["out_x"]
```

```python
import numpy as np
import concourse.bass as bass
from concourse import mybir

f32, i32, i16, bf16 = mybir.dt.float32, mybir.dt.int32, mybir.dt.int16, mybir.dt.bfloat16
ALU = mybir.AluOpType
ACT = mybir.ActivationFunctionType
AX = mybir.AxisListType

P = 128
N, E, C = 6250, 100000, 256
NT = -(-N // P)
NP = NT * P
LAST = N - (NT - 1) * P
GT = 4
NG = -(-NT // GT)
CC = C // P
H, DK = 4, 64
R, T = 8, 4
TABLE_STEPS, MIX_STEPS = 1, 0.57
WINDOW_TILES = 13
SOFTMAX_STEPS = 0.3
WEIGHT_STEPS = 4
START_STEPS = 3
COUNT_TILES = 24
NTS = (N + T * (P - 1)) // P
KQV = 3 * C
CH = 256
HALF = CH // P
NCH = E // CH + (1 if E % CH else 0) + NT - 1
CG = -(-NCH // P)
NCP = CG * P
EP, EF = 125, 800
EPAD = E + CH
BIG = 1e30
LN_EPS, ATT_EPS = 1e-5, 1e-6
FF = 4 * C
FC = FF // P
KK = int(0.5 * N) - 1
KT = -(-KK // P)
KLAST = KK - (KT - 1) * P
AW = C + H


def tiles_of(g):
    return list(range(g * GT, min(NT, (g + 1) * GT)))


class Engine:

    def __init__(self, nc, eng, name):
        self.e, self.sem, self.count, self.seen = eng, nc.alloc_semaphore("done_" + name), 0, {}

    def need(self, *tokens):
        for tok in tokens:
            if tok is None:
                continue
            sem, value = tok
            if self.seen.get(id(sem), 0) < value:
                self.e.wait_ge(sem, value)
                self.seen[id(sem)] = value

    def mark(self, ins):
        self.count += 1
        ins.then_inc(self.sem, 1)
        return (self.sem, self.count)


class Slot:

    def __init__(self, nc, name):
        self.sem, self.value, self.last = nc.alloc_semaphore("dma_" + name), 0, None

    def start(self, eng, ins_of, *tokens):
        eng.need(self.last, *tokens)
        self.value += 16
        ins_of().then_inc(self.sem, 16)
        self.last = (self.sem, self.value)
        return self.last


class Banks:

    def __init__(self, banks):
        self.banks, self.free, self.at = banks, [None] * len(banks), -1

    def take(self, pe):
        self.at = (self.at + 1) % len(self.banks)
        pe.need(self.free[self.at])
        return self.at, self.banks[self.at]


class Inverse:
    RING = 7

    def __init__(self, room, tiles, iota_row, bank, pe, dve):
        self.tiles, self.iota, self.bank, self.pe, self.dve = tiles, iota_row, bank, pe, dve
        R_ = self.RING
        self.col = [room[:, i * P:(i + 1) * P] for i in range(R_)]
        self.row = [room[:, R_ * P + i * tiles:R_ * P + (i + 1) * tiles] for i in range(R_)]
        self.free = [None] * R_

    def add(self, j, slot_mod, slot_div, value, first, last, *ready):
        V, i = self.dve.e, j % self.RING
        self.dve.need(self.free[i], *ready)
        self.dve.mark(V.tensor_scalar(self.col[i], self.iota, slot_mod[:, j:j + 1], None, ALU.is_equal))
        t = self.dve.mark(V.tensor_scalar(self.row[i], self.iota[:, 0:self.tiles], slot_div[:, j:j + 1], value[:, j:j + 1],
                                          ALU.is_equal, ALU.mult))
        self.pe.need(t)
        self.last = self.free[i] = self.pe.mark(self.pe.e.matmul(self.bank[:, 0:self.tiles], lhsT=self.col[i], rhs=self.row[i], start=first, stop=last))
        return self.free[i]


def sort_edges(nc, d_dst, d_row, d_sorted, d_place, d_total, room, iota_row, iota_p, pool, unsorted, *ready):
    G = nc.gpsimd
    BLOCKS = -(-E // P)
    NODES = NP + P
    NF = NODES // P
    work, dma = nc.alloc_semaphore("sort_work"), nc.alloc_semaphore("sort_dma")
    lo = 0

    def part(*shape, dt=None):
        nonlocal lo
        n = int(np.prod(shape))
        ap = room[:, lo:lo + n]
        lo += n
        ap = ap if dt is None else ap.bitcast(dt)
        return ap if len(shape) == 1 else ap.rearrange("p (a b) -> p a b", a=shape[0])

    before, same = part(P), part(2, P)
    other, places, places2 = part(P), part(NF), part(NF)
    d_col, r_col, node, place, moved, target = (part(1) for _ in range(6))
    node_i, target_i = part(1, dt=i32), part(1, dt=i32)
    assert lo <= room.shape[1]

    def step(ins):
        ins.then_inc(work, 1)
        G.wait_ge(work, 1)
        G.sem_clear(work)

    def move(*dmas):
        for i, ins_of in enumerate(dmas):
            ins_of().then_inc(dma, 16)
            G.wait_ge(dma, 16 * (i + 1))
        G.dma_reset(range(dma.num, dma.num + 1))
        G.sem_clear(dma)

    def at_index(i):
        return bass.IndirectOffsetOnAxis(ap=i, axis=0)

    def blocks(put):
        with G.Fori(0, BLOCKS * P, P) as e0:
            move(lambda: G.dma_start(d_col, d_dst[bass.ds(e0, P), :]),
                 lambda: G.dma_start(other, d_dst[bass.ds(e0, P), :].rearrange("(o e) u -> o (e u)", o=1).to_broadcast([P, P])))
            step(G.tensor_scalar(same[:, 0, :], other, d_col, None, ALU.is_equal))
            step(G.tensor_tensor(out=same[:, 1, :], in0=same[:, 0, :], in1=before, op=ALU.mult))
            w = P // 2
            while w:
                step(G.tensor_tensor(out=same[:, :, 0:w], in0=same[:, :, 0:w], in1=same[:, :, w:2 * w], op=ALU.add))
                w //= 2
            step(G.tensor_scalar(node, d_col, float(NP), None, ALU.min))
            step(G.tensor_copy(node_i, node))
            move(lambda: G.indirect_dma_start(place, None, d_place[:, :], at_index(node_i)))
            step(G.tensor_tensor(out=moved, in0=place, in1=same[:, 0, 0:1], op=ALU.add))
            move(lambda: G.indirect_dma_start(d_place[:, :], at_index(node_i), moved, None))
            if put:
                step(G.tensor_tensor(out=target, in0=place, in1=same[:, 1, 0:1], op=ALU.add))
                step(G.tensor_copy(target_i, target))
                move(lambda: G.dma_start(r_col, d_row[bass.ds(e0, P), :]),
                     lambda: G.indirect_dma_start(d_sorted[0][:, :], at_index(target_i), d_col, None),
                     lambda: G.indirect_dma_start(d_sorted[1][:, :], at_index(target_i), r_col, None))

    pool.need(*ready)
    flag = nc.values_load(unsorted[0:1, 0:1], engines=[mybir.EngineType.Pool], min_val=0, max_val=E,
                          skip_runtime_bounds_check_because="it is a count of edges")
    with G.If(flag > 0):
        step(G.tensor_scalar(before, iota_row, iota_p, None, ALU.is_lt))
        step(G.memset(places, 0.0))
        move(lambda: G.dma_start(d_place.rearrange("(p f) u -> p (f u)", p=P), places))
        blocks(False)
        move(lambda: G.dma_start(places, d_place.rearrange("(p f) u -> p (f u)", p=P)))
        step(G.memset(places2[:, 0:1], 0.0))
        step(G.tensor_copy(places2[:, 1:NF], places[:, 0:NF - 1]))
        step(G.tensor_copy(moved, places[:, NF - 1:NF]))
        a, b, w = places2, places, 1
        while w < NF:
            step(G.tensor_copy(b[:, 0:w], a[:, 0:w]))
            step(G.tensor_tensor(out=b[:, w:NF], in0=a[:, w:NF], in1=a[:, 0:NF - w], op=ALU.add))
            a, b, w = b, a, 2 * w
        step(G.tensor_tensor(out=moved, in0=moved, in1=a[:, NF - 1:NF], op=ALU.add))
        move(lambda: G.dma_start(d_total[:, :], moved),
             lambda: G.dma_start(other, d_total.rearrange("(o e) u -> o (e u)", o=1).to_broadcast([P, P])))
        step(G.tensor_tensor(out=other, in0=other, in1=before, op=ALU.mult))
        w = P // 2
        while w:
            step(G.tensor_tensor(out=other[:, 0:w], in0=other[:, 0:w], in1=other[:, w:2 * w], op=ALU.add))
            w //= 2
        step(G.tensor_scalar(a, a, other[:, 0:1], None, ALU.add))
        move(lambda: G.dma_start(d_place.rearrange("(p f) u -> p (f u)", p=P), a))
        blocks(True)
        n = BLOCKS * P
        for i, d in enumerate((d_dst, d_row)):
            move(lambda: G.dma_start(d[0:n, :].rearrange("(p f) u -> p (f u)", p=P), d_sorted[i][0:n, :].rearrange("(p f) u -> p (f u)", p=P)))


def build(nc, x, src, dst, etype, ntype, kW, qW, vW, aW, att, msg, pri, skip, mWq, mWk, mWv, mWm,
          mW1, mW2, g1, b1, g2, b2, wr, br, fw1, fb1, fw2, fb2, out):
    pe, act, dve = Engine(nc, nc.tensor, "pe"), Engine(nc, nc.scalar, "act"), Engine(nc, nc.vector, "dve")
    pool, sp = Engine(nc, nc.gpsimd, "pool"), Engine(nc, nc.sync, "sp")
    V, A, G, TE = nc.vector, nc.scalar, nc.gpsimd, nc.tensor

    d_dst = nc.dram_tensor("edge_dst", (EPAD, 1), f32)
    d_row = nc.dram_tensor("edge_row", (EPAD, 1), f32)
    d_sorted = [nc.dram_tensor("sorted_" + q, (EPAD, 1), f32) for q in ("dst", "row")]
    d_place = nc.dram_tensor("next_place", (NP + P, 1), f32)
    d_total = nc.dram_tensor("block_total", (P, 1), f32)
    d_rel = nc.dram_tensor("chunk_rel", (NCP, CH), bf16)
    d_off = nc.dram_tensor("chunk_off", (2, NCP), i16)
    d_base = nc.dram_tensor("base", (NP, C), f32)
    d_ktab = nc.dram_tensor("k_table", (NP * R, C), f32)
    d_xn = nc.dram_tensor("xn", (NP, C), f32)
    d_kqv = nc.dram_tensor("kqv", (NP + NTS * P, KQV), f32)
    d_pair = nc.dram_tensor("xl_and_sum", (NP, 2 * C), f32)
    d_vtab = nc.dram_tensor("v_table", (NP * R, C), f32)

    ARENA, E_SIZE = 53200, 5400
    arena = nc.alloc_sbuf_tensor("arena", [P, ARENA], f32)
    at = [0]

    def room(n):
        lo = at[0]
        at[0] += n
        assert at[0] <= ARENA, at[0]
        return lo

    def view(lo, n, pat=None, dt=None, **kw):
        ap = arena[:, lo:lo + n]
        if dt is not None:
            ap = ap.bitcast(dt)
        return ap.rearrange(pat, **kw) if pat else ap

    xT = view(room(CC * NP), CC * NP, "p (c n) -> p c n", c=CC)
    lo_big = room((NT + 1) * AW)
    q_all = view(lo_big, (NT + 1) * C)
    acc = view(lo_big, (NT + 1) * AW)
    lo_S = room(H * NCP * HALF)
    S_all = view(lo_S, H * NCP * HALF, "p (h g j c) -> p h g j c", h=H, g=CG, j=HALF)
    S_row = view(lo_S, H * NCP * HALF, "p (h g e) -> p h g e", h=H, g=CG)
    relE = view(room(HALF * NCP // 2), HALF * NCP // 2, "p (g j c) -> p g j c", dt=bf16, g=CG, j=HALF)
    idxE = view(room(HALF * NCP), HALF * NCP, "p (g j c) -> p g j c", dt=i32, g=CG, j=HALF)
    ident, iota_row, ones = view(room(P), P), view(room(P), P), view(room(P), P)
    iota_p = view(room(1), 1)
    lo_flag = room(CG * (CH + 2) // 2)
    flag = view(lo_flag, CG * (CH + 2) // 2, "p (g e) -> p g e", dt=bf16, g=CG)
    offr = view(room(NCP), NCP, dt=i16)[0:1, :]
    lo_cr = room(4 * (NCP // 2))
    small = room(1000)
    lo_E = room(E_SIZE)
    lo_B = room(ARENA - at[0])
    B_SIZE = ARENA - lo_B

    banks = [nc.alloc_psum_tensor(f"bank{i}", [P, 512], f32) for i in range(8)]
    fg, bg = Banks(banks[0:3]), Banks(banks[3:6])
    allb = Banks(banks[0:6])

    t_io = pool.mark(G.iota(iota_row, [[1, P]], base=0, channel_multiplier=0, allow_small_or_imprecise_dtypes=True))
    t_ip = pool.mark(G.iota(iota_p, [[1, 1]], base=0, channel_multiplier=1, allow_small_or_imprecise_dtypes=True))
    dve.need(t_io, t_ip)
    t_id = dve.mark(V.tensor_scalar(ident, iota_row, iota_p, None, ALU.is_equal))
    t_one = dve.mark(V.memset(ones, 1.0))

    def transpose(dst_ps, src_ap):
        return TE.transpose(dst_ps, src_ap, ident)

    def rsqrt(eng_vars, y, tmp, n, tok, between=iter(())):
        dve.need(tok)
        t = dve.mark(V.tensor_scalar(y.bitcast(i32), eng_vars.bitcast(i32), -0.5, float(0x5F3759DF), ALU.mult, ALU.add))
        for _ in range(3):
            dve.need(t)
            t = dve.mark(V.tensor_tensor(out=tmp, in0=y, in1=y, op=ALU.mult))
            dve.need(t)
            next(between, None)
            t = dve.mark(V.scalar_tensor_tensor(out=tmp, in0=tmp, scalar=-0.5, in1=eng_vars, op0=ALU.mult, op1=ALU.mult))
            dve.need(t)
            next(between, None)
            t = dve.mark(V.scalar_tensor_tensor(out=y, in0=tmp, scalar=1.5, in1=y, op0=ALU.add, op1=ALU.mult))
        return t

    sm = [small]

    def tiny(n, dt=None):
        lo = sm[0]
        sm[0] += n
        assert sm[0] <= small + 1000
        ap = arena[:, lo:lo + n]
        return ap if dt is None else ap.bitcast(dt)

    stats = tiny(GT * 6).rearrange("p (t s) -> p t s", s=6)
    mv = tiny(GT * 2).rearrange("p (t s) -> p t s", s=2)
    var, rstd, nt_tmp, shift = tiny(GT), tiny(GT), tiny(GT), tiny(GT)
    g1T, b1T = tiny(CC), tiny(CC)
    priP = tiny(CC * R).rearrange("p (c r) -> p c r", c=CC)
    fb1T = tiny(FC)
    skn, skip_part = tiny(NT), tiny(NT)
    skipP = tiny(T)
    brP = tiny(1)

    def ln_stats(tile_aps, tok, between=iter(())):
        n = len(tile_aps)
        dve.need(tok)
        ts = []
        for i, ap in enumerate(tile_aps):
            ts.append(dve.mark(V.bn_stats(stats[:, i, :], ap)))
        for i in range(n):
            dve.need(ts[i])
            t = dve.mark(V.bn_aggr(mv[:, i, :], stats[:, i, :]))
        dve.need(t)
        t = dve.mark(V.tensor_scalar(var[:, 0:n], mv[:, 0:n, 1], LN_EPS, None, ALU.add))
        return rsqrt(var[:, 0:n], rstd[:, 0:n], nt_tmp[:, 0:n], n, t, between)

    s_small = [Slot(nc, f"small{i}") for i in range(8)]
    nsm = [0]

    def load_small(dst_ap, src_ap, *tok):
        nsm[0] += 1
        return s_small[nsm[0] % 8].start(sp, lambda: nc.sync.dma_start(dst_ap, src_ap, allow_slow_non_contiguous=True), *tok)

    lo = lo_B
    W = [view(lo + c * T * KQV, T * KQV) for c in range(CC)]; lo += CC * T * KQV
    BD = view(lo, CC * R * P, "p (c r n) -> p c r n", c=CC, r=R); lo += CC * R * P
    NGX, NKQV = 4, 3
    xg = [view(lo + i * C, C) for i in range(NGX)]; lo += NGX * C
    xgT = [view(lo + i * C, C, "p (c n) -> p c n", c=CC) for i in range(2)]; lo += 2 * C
    kqv = [view(lo + i * KQV, KQV) for i in range(NKQV)]; lo += NKQV * KQV
    assert lo <= lo_B + B_SIZE
    lo = lo_B
    tabs = [view(lo + i * R * C, R * C, "p (r n) -> p r n", r=R) for i in range(2)]; lo += 2 * R * C
    NZ = 3
    zin = [view(lo + i * C, C) for i in range(NZ)]; lo += NZ * C
    zT = [view(lo + i * C, C, "p (c n) -> p c n", c=CC) for i in range(2)]; lo += 2 * C
    assert lo <= lo_B + CC * T * KQV
    lo = lo_S
    tri = view(lo, P); lo += P
    ntN, ntN_i = view(lo, P)[0:NT, :], view(lo + P, P, dt=i32)[0:NT, :]; lo += 2 * P
    ntP = view(lo, NT); lo += NT
    is_t, before, colsum, colend = (view(lo + i * T * NT, T * NT, "p (t j) -> p t j", t=T) for i in range(4)); lo += 4 * T * NT
    t_cnt, t_tiles, t_first, t_end = (view(lo + i * T, T) for i in range(4)); lo += 4 * T
    t_ti = view(lo, T, dt=i32); lo += T
    slot, slot_i = view(lo, NT), view(lo + NT, NT, dt=i32); lo += 2 * NT
    node_f = view(lo, NT); lo += NT
    slot_mod, slot_div = view(lo, NT), view(lo + NT, NT); lo += 2 * NT
    inv_room = view(lo, Inverse.RING * (P + NTS)); lo += Inverse.RING * (P + NTS)
    node_i, from_i = view(lo, NTS, dt=i32), view(lo + NTS, NTS, dt=i32); lo += 2 * NTS
    w_off, w_cmp = view(lo, NTS), view(lo + NTS, NTS); lo += 2 * NTS
    w_off_i = view(lo, NTS // 2, dt=i16); lo += NTS // 2
    own_row = view(lo, NTS); lo += NTS
    assert lo <= lo_S + 3072

    lo = lo_E
    NX = 3
    xs = [view(lo + i * GT * C, GT * C, "p (t n) -> p t n", t=GT) for i in range(NX)]; lo += NX * GT * C
    xns = [view(lo + i * GT * C, GT * C, "p (t n) -> p t n", t=GT) for i in range(2)]; lo += 2 * GT * C
    assert lo <= lo_E + E_SIZE

    sx = [Slot(nc, f"x{i}") for i in range(NX)]
    sbase = [Slot(nc, f"base{i}") for i in range(2)]

    t_zero = dve.mark(V.memset(xs[(NG - 1) % NX][:, :, :], 0.0))
    dve.need(t_zero)
    t = dve.mark(V.memset(ntN_i, T))
    t_n = [load_small(ntN_i[0:NT - 1, :], ntype[0:(NT - 1) * P].rearrange("(j p) -> j p", p=P), t),
           load_small(ntN_i[NT - 1:NT, 0:LAST], ntype[(NT - 1) * P:N].rearrange("(o p) -> o p", o=1), t)]
    shifts, s_sh = [tiny(2 * GT) for _ in range(2)], [None] * 2
    x_free = [None] * NX
    x_free[(NG - 1) % NX] = t_zero

    def load_x(g):
        i = g % NX
        ts = tiles_of(g)
        if g < NG - 1:
            return sx[i].start(sp, lambda: nc.sync.dma_start(
                xs[i][:, 0:len(ts), :], x[g * 512:g * 512 + len(ts) * P, :].rearrange("(t p) n -> p t n", p=P)), x_free[i])
        return sx[i].start(sp, lambda: nc.sync.dma_start(xs[i][0:LAST, 0, :], x[g * 512:N, :]), x_free[i])

    tx = [None] * NG
    for g in range(NX):
        tx[g] = load_x(g) if not (g == (NG - 1) % NX) else sx[g].start(sp, lambda: nc.sync.dma_start(
            xs[g][:, :, :], x[g * 512:(g + 1) * 512, :].rearrange("(t p) n -> p t n", p=P)), t_zero)
    t_sk = load_small(skipP, skip.rearrange("(o n) -> o n", o=1).to_broadcast([P, T]))
    t_W = [load_small(W[c].rearrange("p (t m) -> p t m", t=T)[:, :, i * C:(i + 1) * C],
                      w_[:, c * P:(c + 1) * P, :].rearrange("t p n -> p t n"))
           for i, w_ in enumerate((kW, qW, vW)) for c in range(CC)]
    zero_rows = kqv[NKQV - 1]
    t_z22 = dve.mark(V.memset(zero_rows, 0.0))
    t_z22 = load_small(d_kqv[N:NP, :], zero_rows[0:NP - N, :], t_z22)
    dve.need(*t_n)
    t = dve.mark(V.tensor_copy(ntN, ntN_i))
    t_tri = dve.mark(V.tensor_scalar(tri, iota_row, iota_p, None, ALU.is_gt))
    pe.need(t, t_id, t_tri, t_one)
    k, bank = allb.take(pe)
    tp = pe.mark(TE.transpose(bank[:, 0:NT], ntN, ident[0:NT, 0:NT]))
    dve.need(tp)
    allb.free[k] = t = dve.mark(V.tensor_copy(ntP, bank[:, 0:NT]))
    dve.need(t)
    for ty in range(T):
        t = dve.mark(V.tensor_scalar(is_t[:, ty, :], ntP, float(ty), None, ALU.is_equal))
    pe.need(t)
    k, bank = allb.take(pe)
    TE.matmul(bank[:, 0:T * NT], lhsT=tri, rhs=is_t, start=True, stop=True)
    k2, bank2 = allb.take(pe)
    tp = pe.mark(TE.matmul(bank2[:, 0:T * NT], lhsT=ones, rhs=is_t, start=True, stop=True))
    dve.need(tp)
    t = dve.mark(V.tensor_copy(before, bank[:, 0:T * NT].rearrange("p (t j) -> p t j", t=T)))
    t2 = allb.free[k] = allb.free[k2] = dve.mark(V.tensor_copy(colsum, bank2[:, 0:T * NT].rearrange("p (t j) -> p t j", t=T)))
    dve.need(t2)
    for ty in range(T):
        t = dve.mark(V.tensor_tensor_scan(out=colend[:, ty, :], data0=colsum[:, ty, :], data1=colsum[:, ty, :], initial=0.0,
                                          op0=ALU.add, op1=ALU.bypass))
    dve.need(t)
    t = dve.mark(V.tensor_scalar(t_ti, colend[:, :, NT - 1], float(P - 1), None, ALU.add))
    dve.need(t)
    t = dve.mark(V.tensor_scalar(t_ti, t_ti, int(np.log2(P)), None, ALU.arith_shift_right))
    dve.need(t)
    t = dve.mark(V.tensor_copy(t_tiles, t_ti))
    dve.need(t)
    t = dve.mark(V.tensor_tensor_scan(out=t_end, data0=t_tiles, data1=t_tiles, initial=0.0, op0=ALU.add, op1=ALU.bypass))
    dve.need(t)
    t = dve.mark(V.tensor_tensor(out=t_first, in0=t_end, in1=t_tiles, op=ALU.subtract))
    t2 = dve.mark(V.tensor_tensor(out=colend, in0=colend, in1=colsum, op=ALU.subtract))
    dve.need(t, t2)
    t = dve.mark(V.tensor_scalar(t_first, t_first, float(P), None, ALU.mult))
    t2 = dve.mark(V.tensor_tensor(out=colend, in0=colend, in1=before, op=ALU.add))
    dve.need(t, t2)
    t = dve.mark(V.tensor_tensor(out=colend, in0=colend, in1=t_first.unsqueeze(2).to_broadcast([P, T, NT]), op=ALU.add))
    dve.need(t)
    t = dve.mark(V.tensor_tensor(out=colend, in0=colend, in1=is_t, op=ALU.mult))
    dve.need(t)
    t = dve.mark(V.tensor_reduce(slot, colend.rearrange("p t j -> p j t"), AX.X, ALU.add))
    dve.need(t)
    t_nf = pool.mark(G.iota(node_f, [[P, NT]], base=1, channel_multiplier=1, allow_small_or_imprecise_dtypes=True))
    t = dve.mark(V.tensor_copy(slot_i, slot))

    def split_slots(slot_i, scratch, *tok):
        dve.need(*tok)
        t = dve.mark(V.tensor_scalar(scratch, slot_i, P - 1, None, ALU.bitwise_and))
        dve.need(t)
        t = dve.mark(V.tensor_copy(slot_mod, scratch))
        dve.need(t)
        t = dve.mark(V.tensor_scalar(scratch, slot_i, int(np.log2(P)), None, ALU.logical_shift_right))
        dve.need(t)
        return dve.mark(V.tensor_copy(slot_div, scratch))

    t_slot = split_slots(slot_i, slot.bitcast(i32), t)
    dve.need(t_nf)
    t_val = dve.mark(V.scalar_tensor_tensor(out=node_f[:, NT - 1:NT], in0=iota_p, scalar=float(LAST), in1=node_f[:, NT - 1:NT],
                                            op0=ALU.is_lt, op1=ALU.mult))
    inv = Inverse(inv_room, NTS, iota_row, banks[7], pe, dve)
    t = dve.mark(V.tensor_scalar(w_off, iota_row[:, 0:NTS], t_end[:, 0:1], None, ALU.is_ge))
    for ty in range(1, T - 1):
        t2 = dve.mark(V.tensor_scalar(w_cmp, iota_row[:, 0:NTS], t_end[:, ty:ty + 1], None, ALU.is_ge))
        dve.need(t, t2)
        t = dve.mark(V.tensor_tensor(out=w_off, in0=w_off, in1=w_cmp, op=ALU.add))
        dve.need(t)
    t_woff = dve.mark(V.tensor_scalar(w_off_i, w_off, float(KQV), None, ALU.mult))

    xn_free = [None, None]
    s_xn = [Slot(nc, f"xn{i}") for i in range(2)]
    pe_read = [None, None]
    t_xT = [None] * NG
    for g in range(NG):
        ts = tiles_of(g)
        n = len(ts)
        xb, xnb = xs[g % NX], xns[g % 2]
        if g == NG - 1:
            dve.need(x_free[g % NX])
            tz = dve.mark(V.memset(xb[:, 0, :], 0.0))
            x_free[g % NX] = tz
            tx[g] = load_x(g)
        inverting = (inv.add(j, slot_mod, slot_div, node_f, j == 0, j == NT - 1, t_slot, t_val) for j in ts)
        t = ln_stats([xb[:, i, :] for i in range(n)], tx[g], inverting)
        dve.need(t, s_sh[g % 2])
        sh = shifts[g % 2]
        t = dve.mark(V.scalar_tensor_tensor(out=sh[:, 0:n], in0=mv[:, 0:n, 0], scalar=-1.0, in1=rstd[:, 0:n], op0=ALU.mult, op1=ALU.mult))
        t2 = dve.mark(V.tensor_copy(sh[:, GT:GT + n], rstd[:, 0:n]))
        act.need(t, t2, xn_free[g % 2], pe_read[g % 2], s_xn[g % 2].last)
        for i in range(n):
            t = s_sh[g % 2] = act.mark(A.activation(xnb[:, i, :], xb[:, i, :], ACT.Identity, bias=sh[:, i:i + 1], scale=sh[:, GT + i:GT + i + 1]))
        pe.need(t, t_id)
        for c in range(CC):
            k, bank = allb.take(pe)
            for i in range(n):
                ins = transpose(bank[:, i * P:(i + 1) * P], xnb[:, i, c * P:(c + 1) * P])
            tp = pe.mark(ins)
            act.need(tp)
            t_xT[g] = allb.free[k] = act.mark(A.copy(xT[:, c, g * 512:g * 512 + n * P], bank[:, 0:n * P]))
        pe_read[g % 2] = tp
        s_xn[g % 2].start(sp, lambda: nc.sync.dma_start(
            d_xn[g * 512:g * 512 + n * P, :].rearrange("(t p) n -> p t n", p=P), xnb[:, 0:n, :]), t)
        for _ in inverting:
            pass
        pool.need(t)
        xn_free[g % 2] = tb = pool.mark(G.tensor_tensor(out=xb[:, 0:n, :], in0=xb[:, 0:n, :], in1=xnb[:, 0:n, :], op=ALU.add))
        x_free[g % NX] = sbase[g % 2].start(sp, lambda: nc.sync.dma_start(
            d_base[g * 512:g * 512 + n * P, :].rearrange("(t p) n -> p t n", p=P), xb[:, 0:n, :]), tb)
        if g + NX < NG - 1:
            tx[g + NX] = load_x(g + NX)
    t_base_all = [s.last for s in sbase]
    act.need(t_sk)
    t = act.mark(A.activation(skipP, skipP, ACT.Exp, scale=-1.0))
    dve.need(t)
    t = dve.mark(V.tensor_scalar(skipP, skipP, 1.0, None, ALU.add))
    dve.need(t)
    t = dve.mark(V.reciprocal(skipP, skipP))
    dve.need(t)
    t = dve.mark(V.tensor_scalar(skn, ntP, 0.0, skipP[:, 0:1], ALU.is_equal, ALU.mult))
    for ty in range(1, T):
        dve.need(t)
        t = dve.mark(V.tensor_scalar(skip_part, ntP, float(ty), skipP[:, ty:ty + 1], ALU.is_equal, ALU.mult))
        dve.need(t)
        t = dve.mark(V.tensor_tensor(out=skn, in0=skn, in1=skip_part, op=ALU.add))
    t_skn = t
    t_xn_all = [s.last for s in s_xn]
    E_free = [xn_free[0], xn_free[1], tp] + t_base_all + t_xn_all

    def load_blocks(rel, *tok):
        dve.need(*tok)
        tz = dve.mark(V.memset(BD[:, :, :, :], 0.0))
        toks = []
        for c in range(CC):
            for h2 in range(2):
                toks.append(load_small(BD[h2 * DK:(h2 + 1) * DK, c, :, h2 * DK:(h2 + 1) * DK],
                                       rel[:, 2 * c + h2, :, :].rearrange("r d e -> d r e"), tz))
        return toks

    tb4 = load_blocks(att)
    for c in range(CC):
        for h2 in range(2):
            t_pri = load_small(priP[h2 * DK:(h2 + 1) * DK, c, :],
                               pri.rearrange("r (h o) -> h o r", o=1)[2 * c + h2].to_broadcast([DK, R]))
            tb4.append(t_pri)
    pe.need(*tb4)
    for c in range(CC):
        for r0 in range(0, R, 4):
            k, bank = allb.take(pe)
            for r in range(r0, r0 + 4):
                ins = transpose(bank[:, (r - r0) * P:(r - r0 + 1) * P], BD[:, c, r, :])
            tp = pe.mark(ins)
            dve.need(tp, *tb4)
            for r in range(r0, r0 + 4):
                t_att = dve.mark(V.tensor_scalar(BD[:, c, r, :], bank[:, (r - r0) * P:(r - r0 + 1) * P],
                                                 priP[:, c, r:r + 1], float(1.0 / np.sqrt(DK)), ALU.mult, ALU.mult))
            allb.free[k] = t_att

    node_v, empty = w_off, w_cmp
    t_ns = pool.mark(G.iota(own_row, [[P, NTS]], base=NP + 1, channel_multiplier=1, allow_small_or_imprecise_dtypes=True))
    dve.need(inv.last, t_ns)
    t = dve.mark(V.tensor_scalar(node_v, banks[7][:, 0:NTS], -1.0, None, ALU.add))
    dve.need(t)
    t = dve.mark(V.scalar_tensor_tensor(out=empty, in0=node_v, scalar=0.0, in1=own_row, op0=ALU.is_lt, op1=ALU.mult))
    dve.need(t)
    t = dve.mark(V.tensor_tensor(out=node_v, in0=node_v, in1=empty, op=ALU.add))
    dve.need(t)
    t_node = dve.mark(V.tensor_copy(node_i, node_v))
    t_from = dve.mark(V.tensor_scalar(from_i, node_v, float(N), None, ALU.min))
    s_xg = [Slot(nc, f"xg{i}") for i in range(NGX)]
    s_kqv = [Slot(nc, f"kqv{i}") for i in range(NKQV)]
    xg_free, xgT_free = [None] * NGX, [None] * 2
    t_xgT, t_kqv = {}, {}

    def at_nodes(nodes, s):
        return bass.IndirectOffsetOnAxis(ap=nodes[:, s:s + 1], axis=0)

    def gather_x(s):
        s_xg[s % NGX].start(pool, lambda: G.indirect_dma_start(xg[s % NGX], None, d_xn[:, :], at_nodes(from_i, s)),
                            t_from, t_node, xg_free[s % NGX], *t_xn_all)

    def turn_x(s):
        pe.need(s_xg[s % NGX].last)
        k, bank = allb.take(pe)
        for c in range(CC):
            ins = transpose(bank[:, c * P:(c + 1) * P], xg[s % NGX][:, c * P:(c + 1) * P])
        tp = xg_free[s % NGX] = pe.mark(ins)
        act.need(tp, xgT_free[s % 2])
        t_xgT[s] = allb.free[k] = act.mark(A.copy(xgT[s % 2], bank[:, 0:C].rearrange("p (c n) -> p c n", c=CC)))

    def typed_sweep():
        for s in range(NGX - 1):
            gather_x(s)
        turn_x(0)
        act.need(t_z22)
        pe.need(t_woff, *t_W)
        for s in range(NTS):
            if s + NGX - 1 < NTS:
                gather_x(s + NGX - 1)
            if s + 1 < NTS:
                turn_x(s + 1)
            if s % 8 == 0:
                _, w_at = nc.values_load_multi_w_load_instructions(
                    w_off_i[0:1, s:min(NTS, s + 8)], engines=[mybir.EngineType.PE], min_val=0, max_val=(T - 1) * KQV,
                    skip_runtime_bounds_check_because="a type is below T")
            out_ = kqv[s % NKQV]
            pe.need(t_xgT[s])
            for lo_, n_ in ((0, 2 * C), (2 * C, C)):
                k, bank = allb.take(pe)
                for c in range(CC):
                    ins = TE.matmul(bank[:, 0:n_], lhsT=xgT[s % 2][:, c, :], rhs=W[c][:, lo_:][:, bass.ds(w_at[s % 8], n_)],
                                    start=c == 0, stop=c == CC - 1)
                tp = pe.mark(ins)
                act.need(tp, s_kqv[s % NKQV].last)
                t = allb.free[k] = act.mark(A.copy(out_[:, lo_:lo_ + n_], bank[:, 0:n_]))
            xgT_free[s % 2] = tp
            s_kqv[s % NKQV].start(pool, lambda: G.indirect_dma_start(d_kqv[:, :], at_nodes(node_i, s), out_, None), t, t_z22)
            yield
        w_free.append(tp)
        t_kqv_all.extend([q.last for q in s_kqv])

    w_free, t_kqv_all = [], []
    typed = typed_sweep()
    for _ in range(COUNT_TILES):
        next(typed)

    s_zin = [Slot(nc, f"zin{i}") for i in range(NZ)]
    s_tab = [Slot(nc, f"table{i}") for i in range(2)]
    tab_last = []

    def make_table(bk, table, col, t_rel, steps):
        zin_free, zT_free, t_zT = [None] * NZ, [None] * 2, {}

        def fetch(j):
            s_zin[j % NZ].start(sp, lambda: nc.sync.dma_start(zin[j % NZ], d_kqv[j * P:(j + 1) * P, col:col + C]),
                                zin_free[j % NZ], *w_free, *t_kqv_all)

        def turn(j):
            pe.need(s_zin[j % NZ].last)
            k, bank = bk.take(pe)
            for c in range(CC):
                ins = transpose(bank[:, c * P:(c + 1) * P], zin[j % NZ][:, c * P:(c + 1) * P])
            tp = zin_free[j % NZ] = pe.mark(ins)
            act.need(tp, zT_free[j % 2], *w_free)
            t_zT[j] = bk.free[k] = act.mark(A.copy(zT[j % 2], bank[:, 0:C].rearrange("p (c n) -> p c n", c=CC)))

        for j in range(NZ):
            fetch(j)
        if steps:
            for _ in range(START_STEPS):
                yield
        turn(0)
        for j in range(NT):
            tb = tabs[j % 2]
            te = []
            if j + 1 < NT:
                turn(j + 1)
            if j + NZ < NT:
                fetch(j + NZ)
            if steps:
                yield
            pe.need(t_zT[j], *t_rel)
            for c in range(CC):
                for half in range(2):
                    k, bank = bk.take(pe)
                    tp = pe.mark(TE.matmul(bank[:, :], lhsT=zT[j % 2][:, c, :],
                                           rhs=BD[:, c, half * 4:half * 4 + 4, :], start=True, stop=True))
                    o, i_ = tb[:, half * 4:half * 4 + 4, c * P:(c + 1) * P], bank[:, :].rearrange("p (r n) -> p r n", r=4)
                    act.need(tp, s_tab[j % 2].last)
                    t_e = act.mark(A.copy(o, i_))
                    bk.free[k] = t_e
                    te.append(t_e)
                if steps:
                    yield
            zT_free[j % 2] = tp
            s_tab[j % 2].start(sp, lambda: nc.sync.dma_start(
                table[j * P * R:(j + 1) * P * R, :].rearrange("(p r) n -> p (r n)", r=R), tb.rearrange("p r n -> p (r n)")), *te)
            yield
        tab_last[:] = [s_tab[0].last, s_tab[1].last, tp]

    lo = lo_E
    ed_i = view(lo, EF, dt=i32)[0:EP, :]; lo += EF
    ed = view(lo, EF)[0:EP, :]; lo += EF
    es_i = view(lo, EF, dt=i32)[0:EP, :]; lo += EF
    et_i = view(lo, EF, dt=i32)[0:EP, :]; lo += EF
    junk = view(lo, EF // 2, dt=bf16)[0:EP, :]; lo += EF // 2
    cnt = view(lo, NT + 1)[0:EP, :]; lo += NT + 1
    nxt_i, nxt = view(lo, 1, dt=i32)[0:EP, :], view(lo + 1, 1)[0:EP, :]; lo += 2
    lo_sort = lo
    t_d = load_small(ed_i, dst.rearrange("(p f) -> p f", p=EP), *E_free)
    t_s = load_small(es_i, src.rearrange("(p f) -> p f", p=EP), *E_free)
    t_t = load_small(et_i, etype.rearrange("(p f) -> p f", p=EP), *E_free)
    dve.need(*E_free)
    t = dve.mark(V.memset(nxt_i, 2 ** 24))
    t_n = load_small(nxt_i[0:EP - 1, :], dst.rearrange("(p f) -> p f", p=EP)[1:EP, 0:1], t)
    dve.need(t_d, t_s, t_t, t_n)
    t = dve.mark(V.tensor_copy(nxt, nxt_i))
    t = dve.mark(V.tensor_copy(ed, ed_i))
    dve.need(t)
    t = dve.mark(V.tensor_tensor(out=junk[:, 0:EF - 1], in0=ed[:, 1:EF], in1=ed[:, 0:EF - 1], op=ALU.is_lt))
    t = dve.mark(V.tensor_tensor(out=junk[:, EF - 1:EF], in0=nxt, in1=ed[:, EF - 1:EF], op=ALU.is_lt))
    dve.need(t)
    t = dve.mark(V.tensor_reduce(cnt[:, NT:NT + 1], junk, AX.X, ALU.add))
    t_er = dve.mark(V.scalar_tensor_tensor(out=ed_i.bitcast(f32), in0=es_i, scalar=float(R), in1=et_i, op0=ALU.mult, op1=ALU.add))
    tw = [load_small(d_dst[0:E, :].rearrange("(p f) o -> p (f o)", p=EP), ed, t),
          load_small(d_row[0:E, :].rearrange("(p f) o -> p (f o)", p=EP), ed_i.bitcast(f32), t_er)]
    padv = tiny(4)
    t1 = dve.mark(V.memset(padv[:, 0:2], float(4 * NP)))
    t2 = dve.mark(V.memset(padv[:, 2:4], 0.0))
    tw.append(load_small(d_dst[E:EPAD, :].rearrange("(p f) o -> p (f o)", p=P), padv[:, 0:2], t1))
    tw.append(load_small(d_row[E:EPAD, :].rearrange("(p f) o -> p (f o)", p=P), padv[:, 2:4], t2))
    tc_ = t
    for b in range(NT):
        dve.need(tc_)
        tc_ = dve.mark(V.tensor_scalar(junk, ed, float(P * (b + 1)), None, ALU.is_lt, ALU.add, accum_out=cnt[:, b:b + 1]))
    NB = NT
    edge_end = tiny(NB)
    n_edge, n_chunk, chunk_end = tiny(NB), tiny(NB), tiny(NB)
    nci = tiny(NB, i32)
    pe.need(tc_, t_one)
    k, bank = allb.take(pe)
    tp = pe.mark(TE.matmul(bank[:, 0:NB + 1], lhsT=ones[0:EP, :], rhs=cnt, start=True, stop=True))
    k_table = make_table(allb, d_ktab, 0, [t_att], False)
    dve.need(tp)
    unsorted = tiny(1, i32)
    t_uns = dve.mark(V.tensor_copy(unsorted, bank[:, NB:NB + 1]))
    t = allb.free[k] = dve.mark(V.tensor_copy(edge_end, bank[:, 0:NB]))
    dve.need(t)
    t = dve.mark(V.tensor_copy(n_edge[:, 0:1], edge_end[:, 0:1]))
    t = dve.mark(V.tensor_tensor(out=n_edge[:, 1:NB], in0=edge_end[:, 1:NB], in1=edge_end[:, 0:NB - 1], op=ALU.subtract))
    dve.need(t)
    t = dve.mark(V.tensor_scalar(nci, n_edge, float(CH - 1), None, ALU.add))
    dve.need(t)
    t = dve.mark(V.tensor_scalar(nci, nci, int(np.log2(CH)), None, ALU.arith_shift_right))
    dve.need(t)
    t = dve.mark(V.tensor_copy(n_chunk, nci))
    dve.need(t)
    t = dve.mark(V.tensor_tensor_scan(out=chunk_end, data0=n_chunk, data1=n_chunk, initial=0.0, op0=ALU.add, op1=ALU.bypass))
    iota_c, c_tile, c_e0, c_c0 = tiny(CG), tiny(CG), tiny(CG), tiny(CG)
    start_i = tiny(CG, i32)
    offs = tiny(CG, i16).rearrange("p (o g) -> p o g", o=2)
    cmp_, pr = tiny(NB), tiny(NB)
    t_ic = pool.mark(G.iota(iota_c, [[P, CG]], base=0, channel_multiplier=1, allow_small_or_imprecise_dtypes=True))
    dve.need(t, t_ic)
    for g in range(CG):
        t = dve.mark(V.tensor_scalar(cmp_, chunk_end, iota_c[:, g:g + 1], None, ALU.is_le))
        dve.need(t)
        t = dve.mark(V.tensor_reduce(c_tile[:, g:g + 1], cmp_, AX.X, ALU.add))
        for q, o in ((n_edge, c_e0), (n_chunk, c_c0)):
            dve.need(t)
            t = dve.mark(V.tensor_tensor(out=pr, in0=cmp_, in1=q, op=ALU.mult))
            dve.need(t)
            t = dve.mark(V.tensor_reduce(o[:, g:g + 1], pr, AX.X, ALU.add))
        dve.need(t)
    t = dve.mark(V.tensor_tensor(out=c_c0, in0=iota_c, in1=c_c0, op=ALU.subtract))
    dve.need(t)
    t = dve.mark(V.tensor_scalar(c_c0, c_c0, float(CH), None, ALU.mult))
    dve.need(t)
    t = dve.mark(V.tensor_tensor(out=c_c0, in0=c_c0, in1=c_e0, op=ALU.add))
    dve.need(t)
    t_start = dve.mark(V.tensor_scalar(start_i, c_c0, float(E), None, ALU.min))
    t = dve.mark(V.tensor_scalar(offs[:, 0, :], c_tile, float(C), None, ALU.mult))
    t_offs = dve.mark(V.tensor_scalar(offs[:, 1, :], c_tile, float(AW), None, ALU.mult))
    t_c = load_small(d_off.rearrange("o (g p) -> p o g", p=P), offs, t_offs)
    t_off = load_small(offr[0:1, :], d_off.rearrange("o (n u) -> u (o n)", u=1), t_c)

    for _ in typed:
        pass
    for _ in range(WINDOW_TILES):
        next(k_table)

    lo = lo_E
    drow = view(lo, CG * CH, "p (g e) -> p g e", g=CG); lo += CG * CH
    irow = view(lo, CG * CH, "p (g e) -> p g e", g=CG); lo += CG * CH
    rel_bf = view(lo, CG * CH // 2, "p (g e) -> p g e", dt=bf16, g=CG); lo += CG * CH // 2
    ctile_p = tiny(CG)
    sort_edges(nc, d_dst, d_row, d_sorted, d_place, d_total, view(lo_sort, lo_E + E_SIZE - lo_sort), iota_row, iota_p,
               pool, unsorted, t_uns, tc_, *tw)
    s_win = [Slot(nc, f"win{i}") for i in range(2 * CG)]
    twin = []
    for g in range(CG):
        for q, (o, d) in enumerate(((drow, d_dst), (irow, d_row))):
            twin.append(s_win[2 * g + q].start(pool, lambda: G.indirect_dma_start(
                o[:, g, :], None, d[:, :], bass.IndirectOffsetOnAxis(ap=start_i[:, g:g + 1], axis=0)),
                t_start, tc_, *tw))
    dve.need(*twin)
    t = dve.mark(V.tensor_scalar(ctile_p, c_tile, float(P), None, ALU.mult))
    dve.need(t)
    for g in range(CG):
        t = dve.mark(V.tensor_scalar(drow[:, g, :], drow[:, g, :], ctile_p[:, g:g + 1], float(P), ALU.subtract, ALU.min))
    dve.need(t)
    t_rb = dve.mark(V.tensor_copy(rel_bf[:, :, :], drow[:, :, :]))
    t_rel = load_small(d_rel.rearrange("(g p) e -> p g e", p=P), rel_bf[:, :, :], t_rb)
    t = dve.mark(V.memset(flag[:, :, :], 0.0))
    dve.need(t)
    tmpf = view(lo, CG * CH, "p (g e) -> p g e", g=CG); lo += CG * CH
    t = dve.mark(V.tensor_tensor(out=tmpf[:, :, 1:CH], in0=drow[:, :, 1:CH], in1=drow[:, :, 0:CH - 1], op=ALU.not_equal))
    dve.need(t)
    t_flag = dve.mark(V.tensor_scalar(flag[:, :, 1:CH], tmpf[:, :, 1:CH], -BIG, None, ALU.mult))
    NQ = 4
    summ = tiny(NQ * CG * H).rearrange("p (q g h) -> p q g h", q=NQ, g=CG)
    unbroken = tiny(CG)
    t = dve.mark(V.tensor_reduce(unbroken, tmpf[:, :, 1:CH], AX.X, ALU.max))
    dve.need(t)
    t = dve.mark(V.tensor_scalar(unbroken, unbroken, -1.0, 1.0, ALU.mult, ALU.add))
    dve.need(t)
    for q, s_ in enumerate((drow[:, :, 0:1], drow[:, :, CH - 1:CH], c_tile.unsqueeze(2), unbroken.unsqueeze(2))):
        t_sum = dve.mark(V.tensor_copy(summ[:, q, :, :], s_.to_broadcast([P, CG, H])))
    pe.need(t_sum)
    for o, s_ in ((relE, drow), (idxE, irow)):
        for g in range(CG):
            k, bank = allb.take(pe)
            for j in range(HALF):
                ins = transpose(bank[:, j * P:(j + 1) * P], s_[:, g, j * P:(j + 1) * P])
            tp = pe.mark(ins)
            dve.need(tp)
            t_edge = allb.free[k] = dve.mark(V.tensor_copy(o[:, g, :, :], bank[:, 0:CH].rearrange("p (j c) -> p j c", j=HALF)))
    CR = [view(b_ + i * NCP, NCP)[0:H, :] for b_ in (lo_S + 3072, lo) for i in range(2)]
    lo += 2 * NCP
    assert lo <= lo_E + E_SIZE

    def to_rows(dst_row, src_pg, *tok):
        pe.need(*tok)
        k, bank = allb.take(pe)
        for g in range(CG):
            ins = transpose(bank[0:H, g * P:(g + 1) * P], src_pg(g))
        tp = pe.mark(ins)
        dve.need(tp)
        allb.free[k] = dve.mark(V.tensor_copy(dst_row, bank[0:H, :]))
        return allb.free[k]

    for q in range(NQ):
        t = to_rows(CR[q], lambda g: summ[:, q, g, :], t_sum)
    rF, rL, rT, rU = CR[0:4]
    eqp, brkA, brkB, eqn = (view(lo_cr + i * NCP // 2, NCP // 2, dt=bf16)[0:H, :] for i in range(4))
    dve.need(t)
    t = dve.mark(V.tensor_tensor(out=brkA[:, 1:], in0=rF[:, 1:], in1=rL[:, :NCP - 1], op=ALU.is_equal))
    t = dve.mark(V.tensor_tensor(out=brkB[:, 1:], in0=rT[:, 1:], in1=rT[:, :NCP - 1], op=ALU.is_equal))
    dve.need(t)
    t = dve.mark(V.memset(eqp[:, 0:1], 0.0))
    t = dve.mark(V.memset(eqn[:, NCP - 1:NCP], 0.0))
    t = dve.mark(V.tensor_tensor(out=eqp[:, 1:], in0=brkA[:, 1:], in1=brkB[:, 1:], op=ALU.mult))
    dve.need(t)
    t = dve.mark(V.tensor_copy(eqn[:, :NCP - 1], eqp[:, 1:]))
    dve.need(t)
    t = dve.mark(V.tensor_tensor(out=brkA, in0=eqp, in1=rU, op=ALU.mult))
    t = dve.mark(V.tensor_tensor(out=brkB, in0=eqn, in1=rU, op=ALU.mult))
    dve.need(t)
    for r_ in (brkA, brkB, eqp, eqn):
        t_cr = dve.mark(V.tensor_scalar(r_, r_, -1.0, BIG, ALU.add, ALU.mult))

    t_qz = dve.mark(V.memset(q_all[:, NT * C:(NT + 1) * C], 0.0))
    Q_PART, t_q, j = 7, [], 0
    for i, _ in enumerate(k_table):
        if i % 3 == 0 and j < NT:
            n = min(Q_PART, NT - j)
            t_q.append(load_small(q_all[:, j * C:(j + n) * C].rearrange("p (j n) -> p j n", j=n),
                                  d_kqv[j * P:(j + n) * P, C:2 * C].rearrange("(j p) n -> p j n", p=P), *t_kqv_all))
            j += n
    assert j == NT
    k_done = list(tab_last)

    def background():
        tb_ = load_blocks(msg, *k_done)
        for _ in range(START_STEPS):
            yield
        yield from make_table(bg, d_vtab, 2 * C, tb_, True)
        v_done.extend(tab_last)
        yield from mix()

    v_done = []
    mix_done = []

    def elu1(o, ps, tmp, tok, free):
        act.need(tok, free)
        act.mark(A.activation(tmp, ps, ACT.Exp))
        t = act.mark(A.activation(o, ps, ACT.Relu))
        dve.need(t)
        return t, dve.mark(V.scalar_tensor_tensor(out=o, in0=tmp, scalar=1.0, in1=o, op0=ALU.min, op1=ALU.add))

    def normalise(o, tiles_, tok, free):
        n = len(tiles_)
        dve.need(tok)
        for i in range(n):
            t = dve.mark(V.bn_stats(stats[:, i, :], tiles_[i][1][:, tiles_[i][2] * C:(tiles_[i][2] + 1) * C]))
            if i == 1:
                yield
        dve.need(t)
        for i in range(n):
            t = dve.mark(V.bn_aggr(mv[:, i, :], stats[:, i, :]))
        dve.need(t)
        t = dve.mark(V.tensor_scalar(var[:, 0:n], mv[:, 0:n, 1], LN_EPS, None, ALU.add))
        yield
        t = rsqrt(var[:, 0:n], rstd[:, 0:n], nt_tmp[:, 0:n], n, t)
        dve.need(t)
        t = dve.mark(V.scalar_tensor_tensor(out=shift[:, 0:n], in0=mv[:, 0:n, 0], scalar=-1.0, in1=rstd[:, 0:n], op0=ALU.mult, op1=ALU.mult))
        act.need(t, free)
        for i, (k, bank, j) in enumerate(tiles_):
            t = bg.free[k] = act.mark(A.activation(o[:, i, :], bank[:, j * C:(j + 1) * C], ACT.Identity,
                                                   bias=shift[:, i:i + 1], scale=rstd[:, i:i + 1]))
        normed[0] = t
        yield

    normed = [None]

    def mix():
        HM = 32
        lo = lo_B
        WKV = view(lo, CC * 2 * C, "p (c n) -> p c n", c=CC); lo += CC * 2 * C
        WQ = view(lo, CC * C, "p (c n) -> p c n", c=CC); lo += CC * C
        WM = view(lo, CC * C, "p (c n) -> p c n", c=CC); lo += CC * C
        W1 = view(lo, 4 * 512, "p (c n) -> p c n", c=4); lo += 4 * 512
        W2 = view(lo, 4 * C, "p (c n) -> p c n", c=4); lo += 4 * C
        g2row, b2row = view(lo, C), view(lo + C, C); lo += 2 * C
        QT = view(lo, CC * 512, "p (c n) -> p c n", c=CC); lo += CC * 512
        HC = P // HM
        KVX = view(lo, CC * (P + HC), "p (c n) -> p c n", c=CC); lo += CC * (P + HC)
        zn = view(lo, GT * CC * HC, "p (t c h) -> p t c h", t=GT, c=CC); lo += GT * CC * HC
        bmask = view(lo, P); lo += P
        mT = view(lo, CC * 512, "p (c n) -> p c n", c=CC); lo += CC * 512
        lo_h = lo
        hT = view(lo, 4 * 512, "p (c n) -> p c n", c=4); lo += 4 * 512
        base = view(lo, GT * C, "p (t n) -> p t n", t=GT); lo += GT * C
        xh = view(lo, GT * C, "p (t n) -> p t n", t=GT); lo += GT * C
        assert lo <= lo_B + B_SIZE, (lo - lo_B, B_SIZE)
        Kb = [view(lo_h + i * C, C) for i in range(2)]
        Tb = [view(lo_h + 2 * C + i * C, C) for i in range(2)]
        VX = P + 1
        Vb = [view(lo_h + 4 * C + i * CC * VX, CC * VX, "p (c n) -> p c n", c=CC) for i in range(2)]
        tw_ = [load_small(WKV[:, :, 0:C], mWk.rearrange("(c p) n -> p c n", p=P), *v_done),
               load_small(WKV[:, :, C:2 * C], mWv.rearrange("(c p) n -> p c n", p=P), *v_done),
               load_small(WQ, mWq.rearrange("(c p) n -> p c n", p=P), *v_done),
               load_small(WM, mWm.rearrange("(c p) n -> p c n", p=P), *v_done),
               load_small(W1, mW1.rearrange("(c p) n -> p c n", p=P), *v_done),
               load_small(W2, mW2.rearrange("(c p) n -> p c n", p=P), *v_done),
               load_small(g2row, g2.rearrange("(o n) -> o n", o=1).to_broadcast([P, C]), *v_done),
               load_small(b2row, b2.rearrange("(o n) -> o n", o=1).to_broadcast([P, C]), *v_done),
               load_small(g1T, g1.rearrange("(c p) -> p c", p=P)),
               load_small(b1T, b1.rearrange("(c p) -> p c", p=P))]
        dve.need(*v_done)
        for i in range(2):
            for c in range(CC):
                t = dve.mark(V.memset(Vb[i][:, c, P:VX], 1.0))
        t = dve.mark(V.memset(bmask, 0.0))
        dve.need(t)
        for b in range(P // HM):
            t_bm = dve.mark(V.memset(bmask[b * HM:(b + 1) * HM, b * HM:(b + 1) * HM], 1.0))
        for _ in range(WEIGHT_STEPS):
            yield
        k_free = [t_bm, t_bm]
        pe.need(*tw_)
        for tile in range(NT):
            rows = P if tile < NT - 1 else LAST
            i = tile % 2
            k, bank = bg.take(pe)
            for c in range(CC):
                ins = TE.matmul(bank[:, :], lhsT=xT[:, c, tile * P:(tile + 1) * P], rhs=WKV[:, c, :], start=c == 0, stop=c == CC - 1)
            tp = pe.mark(ins)
            act.need(tp, k_free[i])
            tv = act.mark(A.copy(Vb[i][:, :, 0:P], bank[:, C:2 * C].rearrange("p (c n) -> p c n", c=CC)))
            bg.free[k], tk = elu1(Kb[i], bank[:, 0:C], Tb[i], tv, k_free[i])
            yield
            pe.need(tk, tv)
            for c in range(CC):
                ins = TE.matmul(banks[6 + c][:, 0:VX], lhsT=Kb[i][0:rows, c * P:(c + 1) * P], rhs=Vb[i][0:rows, c, :],
                                start=tile == 0, stop=tile == NT - 1)
            k_free[i] = tkv = pe.mark(ins)
            yield
        dve.need(tkv)
        for c in range(CC):
            t = dve.mark(V.scalar_tensor_tensor(out=KVX[:, c, 0:P], in0=banks[6 + c][:, 0:P], scalar=1.0 / N, in1=bmask, op0=ALU.mult, op1=ALU.mult))
            t_kv = dve.mark(V.tensor_scalar(KVX[:, c, P:], bmask[:, ::HM], banks[6 + c][:, P:VX], None, ALU.mult))
        yield
        base_free = q_free = x_free_ = mT_free = h_free = tb_ = None
        s_b, s_bw = Slot(nc, "base_in"), Slot(nc, "base_out")
        h_free = tkv
        for g in range(NG):
            n = len(tiles_of(g))
            w = n * P
            cols = slice(g * 512, g * 512 + w)
            rows_d = d_base[g * 512:g * 512 + w, :].rearrange("(t p) n -> p t n", p=P)
            tb_ = s_b.start(sp, lambda: nc.sync.dma_start(base[:, 0:n, :], rows_d), base_free, *t_base_all)
            for c in range(CC):
                k, bank = bg.take(pe)
                for kc in range(CC):
                    ins = TE.matmul(bank[:, 0:w], lhsT=WQ[:, kc, c * P:(c + 1) * P], rhs=xT[:, kc, cols], start=kc == 0, stop=kc == CC - 1)
                tp = pe.mark(ins)
                act.need(q_free)
                bg.free[k], tq = elu1(QT[:, c, 0:w], bank[:, 0:w], hT[:, c, 0:w], tp, h_free if c == 0 else None)
                yield
            pe.need(tq, t_kv)
            dve.need(x_free_)
            for i4 in range(n):
                k, bank = bg.take(pe)
                for c in range(CC):
                    ins = TE.matmul(bank[:, c * (P + HC):(c + 1) * (P + HC)], lhsT=QT[:, c, i4 * P:(i4 + 1) * P], rhs=KVX[:, c, :],
                                    start=True, stop=True)
                q_free = tp = pe.mark(ins)
                both = bank[:, 0:CC * (P + HC)].rearrange("p (c n) -> p c n", c=CC)
                dve.need(tp)
                t = dve.mark(V.tensor_scalar(zn[:, i4], both[:, :, P:], ATT_EPS, None, ALU.add))
                dve.need(t)
                t = dve.mark(V.reciprocal(zn[:, i4], zn[:, i4]))
                dve.need(t)
                for c in range(CC):
                    tm = bg.free[k] = dve.mark(V.scalar_tensor_tensor(
                        out=xh[:, i4, c * P:(c + 1) * P].rearrange("p (h d) -> p h d", h=HC), in0=both[:, c, 0:P].rearrange("p (h d) -> p h d", h=HC),
                        scalar=float(N), in1=zn[:, i4, c, :].unsqueeze(2).to_broadcast([P, HC, HM]), op0=ALU.mult, op1=ALU.mult))
                if i4 % 2:
                    yield
            pe.need(tm)
            for c in range(CC):
                k, bank = bg.take(pe)
                for i4 in range(n):
                    ins = transpose(bank[:, i4 * P:(i4 + 1) * P], xh[:, i4, c * P:(c + 1) * P])
                x_free_ = tp = pe.mark(ins)
                act.need(tp, tq)
                tm = bg.free[k] = act.mark(A.copy(hT[:, c, 0:w], bank[:, 0:w]))
            yield
            pe.need(tm)
            kb, tps = [], []
            for i0 in range(0, n, 2):
                k, bank = bg.take(pe)
                for i4 in range(i0, min(n, i0 + 2)):
                    for c in range(CC):
                        ins = TE.matmul(bank[:, (i4 - i0) * C:(i4 - i0 + 1) * C], lhsT=hT[:, c, i4 * P:(i4 + 1) * P], rhs=WM[:, c, :],
                                        start=c == 0, stop=c == CC - 1)
                tps.append(pe.mark(ins))
                kb += [(k, bank, j) for j in range(min(n, i0 + 2) - i0)]
                yield
            h_free = tps[-1]
            yield from normalise(xh, kb, tps[-1], x_free_)
            pe.need(normed[0])
            for c in range(CC):
                k, bank = bg.take(pe)
                for i4 in range(n):
                    ins = transpose(bank[:, i4 * P:(i4 + 1) * P], xh[:, i4, c * P:(c + 1) * P])
                x_free_ = tp = pe.mark(ins)
                act.need(tp, mT_free, *tw_)
                tmt = bg.free[k] = act.mark(A.activation(mT[:, c, 0:w], bank[:, 0:w], ACT.Identity, bias=b1T[:, c:c + 1], scale=g1T[:, c:c + 1]))
            yield
            pe.need(tmt)
            for oc in range(4):
                k, bank = bg.take(pe)
                for kc in range(4):
                    rhs = xT[:, kc, cols] if kc < CC else mT[:, kc - CC, 0:w]
                    ins = TE.matmul(bank[:, 0:w], lhsT=W1[:, kc, oc * P:(oc + 1) * P], rhs=rhs, start=kc == 0, stop=kc == 3)
                tp = pe.mark(ins)
                act.need(tp, h_free)
                th = bg.free[k] = act.mark(A.activation(hT[:, oc, 0:w], bank[:, 0:w], ACT.Relu))
                yield
            mT_free = tp
            pe.need(th)
            kb = []
            for i0 in range(0, n, 2):
                k, bank = bg.take(pe)
                for i4 in range(i0, min(n, i0 + 2)):
                    for kc in range(4):
                        ins = TE.matmul(bank[:, (i4 - i0) * C:(i4 - i0 + 1) * C], lhsT=hT[:, kc, i4 * P:(i4 + 1) * P], rhs=W2[:, kc, :],
                                        start=kc == 0, stop=kc == 3)
                tp = pe.mark(ins)
                kb += [(k, bank, j) for j in range(min(n, i0 + 2) - i0)]
                yield
            h_free = tp
            yield from normalise(xh, kb, tp, x_free_)
            dve.need(normed[0], tb_, *tw_)
            t = dve.mark(V.tensor_tensor(out=xh[:, 0:n, :], in0=xh[:, 0:n, :], in1=g2row.unsqueeze(1).to_broadcast([P, n, C]), op=ALU.mult))
            yield
            dve.need(t)
            t = dve.mark(V.tensor_tensor(out=xh[:, 0:n, :], in0=xh[:, 0:n, :], in1=b2row.unsqueeze(1).to_broadcast([P, n, C]), op=ALU.add))
            yield
            dve.need(t)
            t = dve.mark(V.tensor_tensor(out=base[:, 0:n, :], in0=base[:, 0:n, :], in1=xh[:, 0:n, :], op=ALU.add))
            x_free_ = t
            base_free = s_bw.start(sp, lambda: nc.sync.dma_start(rows_d, base[:, 0:n, :]), t)
            yield
        mix_done.extend([base_free, h_free, x_free_, mT_free, th, tmt])

    lo = lo_E
    NR = 5
    ring = [view(lo + i * HALF * C, HALF * C, "p (j n) -> p j n", j=HALF) for i in range(NR)]; lo += NR * HALF * C
    lo_E2 = lo
    RB = 4
    relB = [view(lo + i * RB * CH // 2, RB * CH // 2, "p (k e) -> p k e", dt=bf16, k=RB) for i in range(2)]; lo += RB * CH
    oh = [view(lo + i * CH, CH) for i in range(3)]; lo += 3 * CH
    prod = [view(lo + i * HALF * C, HALF * C) for i in range(1)]; lo += HALF * C
    assert lo <= lo_E + E_SIZE
    s_ring = [[Slot(nc, f"gather{i}_{j}") for j in range(HALF)] for i in range(NR)]
    s_relB = [Slot(nc, f"relB{i}") for i in range(2)]
    ring_free = [None] * NR
    tabtok = []
    got = {}

    def gather(i, table):
        g, c = divmod(i, P)
        s = i % NR
        toks = []
        for j in range(HALF):
            toks.append(s_ring[s][j].start(pool, lambda: G.indirect_dma_start(
                ring[s][:, j, :], None, table[:, :], bass.IndirectOffsetOnAxis(ap=idxE[:, g, j, c:c + 1], axis=0)),
                t_edge, t_cr, ring_free[s], *tabtok))
        got[i] = toks

    work = background()
    credit = [0.0]

    def advance(steps):
        credit[0] += steps
        while credit[0] >= 1:
            credit[0] -= 1
            next(work, None)

    tabtok[:] = k_done
    LOOK = NR - 1
    relB_free = [None, None]
    t_relB = [None, None]

    def load_relB(kb):
        s = kb % 2
        n = min(RB, NCH - kb * RB)
        t_relB[s] = s_relB[s].start(sp, lambda: nc.sync.dma_start(
            relB[s][:, 0:n, :], d_rel[kb * RB:kb * RB + n, :].rearrange("(o k) e -> o (k e)", o=1).to_broadcast([P, n * CH])),
            t_rel, t_edge, t_cr, relB_free[s])

    load_relB(0)
    load_relB(1)
    for i in range(min(LOOK, NCH)):
        gather(i, d_ktab)
    oh_free, prod_free = [t_cr] * 3, [t_cr] * 2
    t_oh = {}
    reg_batch = {}

    def offsets(i, row, eng, limit):
        if i % 8 == 0:
            n = min(8, NCP - i)
            _, vals = nc.values_load_multi_w_load_instructions(
                offr[0:1, row * NCP + i:row * NCP + i + n], engines=[eng], min_val=0, max_val=limit,
                skip_runtime_bounds_check_because="a chunk's tile is at most the number of tiles")
            reg_batch[eng] = vals
        return reg_batch[eng][i % 8]

    def make_oh(i):
        s, b = i % 3, (i // RB) % 2
        dve.need(t_relB[b], oh_free[s])
        t_oh[i] = dve.mark(V.tensor_scalar(oh[s], relB[b][:, i % RB, :], iota_p, None, ALU.is_equal))
        if i % RB == RB - 1 or i == NCH - 1:
            relB_free[b] = t_oh[i]
            if (i // RB + 2) * RB < NCH:
                load_relB(i // RB + 2)

    make_oh(0)
    make_oh(1)
    pe.need(t_off, t_qz, *t_q, *k_done)
    t_sc = t_cr
    for i in range(NCH):
        g, c = divmod(i, P)
        if i + LOOK < NCH:
            gather(i + LOOK, d_ktab)
        k, bank = fg.take(pe)
        off = offsets(i, 0, mybir.EngineType.PE, NT * C)
        pe.need(t_oh[i])
        for j in range(HALF):
            ins = TE.matmul(bank[:, j * C:(j + 1) * C], lhsT=oh[i % 3][:, j * P:(j + 1) * P],
                            rhs=q_all[:, bass.ds(off, C)], start=True, stop=True)
        oh_free[i % 3] = tp = pe.mark(ins)
        if i + 2 < NCH:
            make_oh(i + 2)
        pr_ = prod[0]
        dve.need(tp, *got[i], t_sc)
        t = fg.free[k] = ring_free[i % NR] = dve.mark(V.tensor_tensor(out=pr_, in0=bank[:, :], in1=ring[i % NR].rearrange("p j n -> p (j n)"), op=ALU.mult))
        dve.need(t)
        t_sc = dve.mark(V.tensor_reduce(S_all[:, :, g, :, c].rearrange("p h j -> p j h"),
                                        pr_.rearrange("p (j h d) -> p j h d", j=HALF, h=H), AX.X, ALU.add))
        advance(MIX_STEPS if v_done else TABLE_STEPS)

    while not v_done:
        advance(1)
    tabtok[:] = v_done
    for i in range(LOOK):
        gather(i, d_vtab)

    lastc = NCH - (CG - 1) * P
    tz = dve.mark(V.memset(S_all[:, :, CG - 1, :, lastc:P], 0.0))
    lo = lo_E2
    F = [view(lo + i * CH, CH) for i in range(4)]; lo += 4 * CH
    LM = view(lo, CG * H, "p (g h) -> p g h", g=CG); lo += CG * H
    FM = view(lo, CG * H, "p (g h) -> p g h", g=CG); lo += CG * H
    cF = view(lo, CG * H, "p (g h) -> p g h", g=CG); lo += CG * H
    cB = view(lo, CG * H, "p (g h) -> p g h", g=CG); lo += CG * H
    pe.need(t_sc, tz)
    for h in range(H):
        for g in range(CG):
            k, bank = fg.take(pe)
            for j in range(HALF):
                ins = transpose(bank[:, j * P:(j + 1) * P], S_all[:, h, g, j, :])
            tp = pe.mark(ins)
            act.need(tp)
            t_tr = fg.free[k] = act.mark(A.copy(S_row[:, h, g, :], bank[:, 0:CH]))
        advance(SOFTMAX_STEPS)
    dve.need(t_tr, tp)
    n_ = 0
    ff = [None] * 4
    for h in range(H):
        for g in range(CG):
            a, b = F[2 * (n_ % 2)], F[2 * (n_ % 2) + 1]
            t = dve.mark(V.tensor_tensor_scan(out=a, data0=flag[:, g, 0:CH], data1=S_row[:, h, g, :], initial=-BIG, op0=ALU.add, op1=ALU.max))
            dve.need(t)
            t = dve.mark(V.tensor_copy(LM[:, g, h:h + 1], a[:, CH - 1:CH]))
            t = dve.mark(V.tensor_tensor_scan(out=b[:, ::-1], data0=flag[:, g, 1:CH + 1][:, ::-1], data1=a[:, ::-1], initial=-BIG, op0=ALU.add, op1=ALU.max))
            dve.need(t)
            t = dve.mark(V.tensor_copy(FM[:, g, h:h + 1], b[:, 0:1]))
            n_ += 1
            advance(SOFTMAX_STEPS)
    rFM, rLM, rCF, rCB = (view(lo_big + i * NCP, NCP)[0:H, :] for i in range(4))
    allb = Banks(banks[0:2])
    allb.free = list(fg.free[0:2])
    t1 = to_rows(rLM, lambda g: LM[:, g, :], t)
    t2 = to_rows(rFM, lambda g: FM[:, g, :], t)
    dve.need(t1, t2)
    t = dve.mark(V.tensor_tensor_scan(out=rLM, data0=brkA, data1=rLM, initial=-BIG, op0=ALU.add, op1=ALU.max))
    t = dve.mark(V.tensor_tensor_scan(out=rFM[:, ::-1], data0=brkB[:, ::-1], data1=rFM[:, ::-1], initial=-BIG, op0=ALU.add, op1=ALU.max))
    dve.need(t)
    t = dve.mark(V.memset(rCF[:, 0:1], -BIG))
    t = dve.mark(V.memset(rCB[:, NCP - 1:NCP], -BIG))
    t = dve.mark(V.tensor_tensor(out=rCF[:, 1:], in0=rLM[:, :NCP - 1], in1=eqp[:, 1:], op=ALU.add))
    t = dve.mark(V.tensor_tensor(out=rCB[:, :NCP - 1], in0=rFM[:, 1:], in1=eqn[:, :NCP - 1], op=ALU.add))
    pe.need(t)
    for o, r_ in ((cF, rCF), (cB, rCB)):
        k, bank = allb.take(pe)
        for g in range(CG):
            ins = TE.transpose(bank[:, g * H:(g + 1) * H], r_[:, g * P:(g + 1) * P], ident[0:H, 0:H])
        tp = pe.mark(ins)
        dve.need(tp)
        t = allb.free[k] = dve.mark(V.tensor_copy(o[:, :, :], bank[:, 0:CG * H].rearrange("p (g h) -> p g h", g=CG)))
    fg.free[0:2] = allb.free
    dve.need(t)
    n_ = 0
    for h in range(H):
        for g in range(CG):
            a, b = F[2 * (n_ % 2)], F[2 * (n_ % 2) + 1]
            t = dve.mark(V.tensor_tensor_scan(out=a, data0=flag[:, g, 0:CH], data1=S_row[:, h, g, :], initial=cF[:, g, h:h + 1], op0=ALU.add, op1=ALU.max))
            dve.need(t)
            t = dve.mark(V.tensor_tensor_scan(out=b[:, ::-1], data0=flag[:, g, 1:CH + 1][:, ::-1], data1=a[:, ::-1], initial=cB[:, g, h:h + 1], op0=ALU.add, op1=ALU.max))
            dve.need(t)
            t = dve.mark(V.tensor_tensor(out=S_row[:, h, g, :], in0=S_row[:, h, g, :], in1=b, op=ALU.subtract))
            act.need(t)
            tx_ = act.mark(A.activation(S_row[:, h, g, :], S_row[:, h, g, :], ACT.Exp))
            pe.need(tx_)
            k, bank = fg.take(pe)
            for j in range(HALF):
                ins = transpose(bank[:, j * P:(j + 1) * P], S_row[:, h, g, j * P:(j + 1) * P])
            tp = pe.mark(ins)
            act.need(tp)
            t_ex = fg.free[k] = act.mark(A.copy(S_all[:, h, g, :, :], bank[:, 0:CH].rearrange("p (j c) -> p j c", j=HALF)))
            n_ += 1
            advance(SOFTMAX_STEPS)

    lo = lo_E2
    so = [view(lo + i * HALF * P, HALF * P) for i in range(3)]; lo += 3 * HALF * P
    Rv = [view(lo + i * HALF * AW, HALF * AW, "p (j n) -> p j n", j=HALF) for i in range(3)]; lo += 3 * HALF * AW
    assert lo <= lo_E + E_SIZE
    t_z = dve.mark(V.memset(acc, 0.0))
    dve.need(t_ex, t_z, t_off)
    so_free, r_free = [None] * 3, [None] * 3
    t_acc = t_z
    pend = []

    def finish_chunk(i, k, bank, tp):
        nonlocal t_acc
        off = offsets(i, 1, mybir.EngineType.DVE, NT * AW)
        dve.need(tp, t_acc)
        t_acc = fg.free[k] = dve.mark(V.tensor_tensor(out=acc[:, bass.ds(off, AW)], in0=acc[:, bass.ds(off, AW)], in1=bank[:, 0:AW], op=ALU.add))

    t_in = {}

    def weigh(i):
        g, c = divmod(i, P)
        s = i % 3
        dve.need(so_free[s])
        t_so = dve.mark(V.tensor_tensor(out=so[s].rearrange("p (j n) -> p j n", j=HALF), in0=iota_row.unsqueeze(1).to_broadcast([P, HALF, P]),
                                        in1=relE[:, g, :, c:c + 1].to_broadcast([P, HALF, P]), op=ALU.is_equal))
        ex = S_all[:, :, g, :, c].rearrange("p h j -> p j h")
        dve.need(*got[i])
        t_r = ring_free[i % NR] = dve.mark(V.tensor_tensor(
            out=Rv[s][:, :, 0:C].rearrange("p j (h d) -> p j h d", h=H), in0=ring[i % NR].rearrange("p j (h d) -> p j h d", h=H),
            in1=ex.unsqueeze(3).to_broadcast([P, HALF, H, DK]), op=ALU.mult))
        act.need(r_free[s], t_ex, t_z)
        t_a = act.mark(A.copy(Rv[s][:, :, C:AW], ex))
        t_in[i] = (t_r, t_a, t_so)

    weigh(0)
    for i in range(NCH):
        s = i % 3
        if i + LOOK < NCH:
            gather(i + LOOK, d_vtab)
        if i + 1 < NCH:
            weigh(i + 1)
        pe.need(*t_in[i])
        k, bank = fg.take(pe)
        for j in range(HALF):
            ins = TE.matmul(bank[:, 0:AW], lhsT=so[s][:, j * P:(j + 1) * P], rhs=Rv[s][:, j, :], start=j == 0, stop=j == HALF - 1)
        so_free[s] = r_free[s] = tp = pe.mark(ins)
        pend.append((i, k, bank, tp))
        if len(pend) > 1:
            finish_chunk(*pend.pop(0))
        advance(MIX_STEPS)
    finish_chunk(*pend.pop(0))
    for _ in work:
        pass

    ALLB = Banks(banks)
    ALLB.free = [t_acc] * 8
    t_a = t_in[NCH - 1][1]
    done = [t_acc, tp, t_a] + mix_done
    pe.need(*done)
    lo = lo_B
    Wa = view(lo, T * CC * C, "p (t c n) -> p t c n", t=T, c=CC); lo += T * CC * C
    F1 = view(lo, CC * FF, "p (c n) -> p c n", c=CC); lo += CC * FF
    F2 = view(lo, FC * C, "p (c n) -> p c n", c=FC); lo += FC * C
    hF = view(lo, FC * 512, "p (c n) -> p c n", c=FC); lo += FC * 512
    fb2row = view(lo, C); lo += C
    assert lo <= lo_B + B_SIZE
    lo = lo_S
    wS, wsel, slot, slot_i = view(lo, NT), view(lo + NT, NT), view(lo + 2 * NT, NT), view(lo + 3 * NT, NT, dt=i32); lo += 4 * NT
    key, khi, klo, eqm, cum, colt, selv, lower = (view(lo + i * NT, NT) for i in range(8)); lo += 8 * NT
    RADIX = 16
    thr, need_ = view(lo, 1), view(lo + 1, 1); lo += 2
    cand, cntp, reach = (view(lo + i * RADIX, RADIX - 1) for i in range(3)); lo += 3 * RADIX
    cmpv = view(lo, (RADIX - 1) * NT, "p (r n) -> p r n", r=RADIX - 1); lo += (RADIX - 1) * NT
    tri, node_f = view(lo, P), view(lo + P, NT); lo += P + NT
    picked = view(lo, KT, dt=i32); lo += KT
    slot_mod, slot_div = view(lo, NT), view(lo + NT, NT); lo += 2 * NT
    inv_room = view(lo, Inverse.RING * (P + KT)); lo += Inverse.RING * (P + KT)
    assert lo <= lo_S + H * NCP * HALF
    lo = 0
    NX1 = 3
    ag = [view(lo + i * GT * C, GT * C, "p (t n) -> p t n", t=GT) for i in range(2)]; lo += 2 * GT * C
    x1 = [view(lo + i * GT * C, GT * C, "p (t n) -> p t n", t=GT) for i in range(NX1)]; lo += NX1 * GT * C
    pair = [view(lo + i * GT * 2 * C, GT * 2 * C, "p (t n) -> p t n", t=GT) for i in range(2)]; lo += 2 * GT * 2 * C
    NMA = 3
    MA = [view(lo + i * CC * T * P, CC * T * P, "p (t c n) -> p t c n", t=T, c=CC) for i in range(NMA)]; lo += NMA * CC * T * P
    rden = view(lo, GT * H, "p (t h) -> p t h", t=GT); lo += GT * H
    assert lo <= CC * NP
    lo = lo_E
    ntr2 = [view(lo + i * 512, 512, dt=i32) for i in range(2)]; lo += 1024
    xlT = view(lo, CC * 512, "p (c n) -> p c n", c=CC); lo += CC * 512
    aT = [view(lo + i * C, C, "p (c n) -> p c n", c=CC) for i in range(NMA)]; lo += NMA * C
    wrrow, wr_prod = view(lo, C), view(lo + C, C); lo += 2 * C
    assert lo <= lo_E + E_SIZE
    s_b2 = [Slot(nc, f"x1in{i}") for i in range(NX1)]
    s_nt2 = [Slot(nc, f"nt2_{i}") for i in range(2)]
    s_pair, s_out = [Slot(nc, f"pair{i}") for i in range(2)], [Slot(nc, f"out{i}") for i in range(2)]
    x1_free, nt_free = [None] * NX1, [None] * 2
    ag_free, ma_free = [None] * 2, [None] * NMA
    accv = acc.rearrange("p (t n) -> p t n", n=AW)

    def rows_of(d, g):
        return d[g * 512:g * 512 + len(tiles_of(g)) * P, :].rearrange("(t p) n -> p t n", p=P)

    def load_group(g):
        n, s = len(tiles_of(g)), g % 2
        valid = min(N - g * 512, n * P)
        s_b2[g % NX1].start(sp, lambda: nc.sync.dma_start(x1[g % NX1][:, 0:n, :], rows_of(d_base, g)), x1_free[g % NX1], *done)
        s_nt2[s].start(sp, lambda: nc.sync.dma_start(
            ntr2[s][:, 0:valid], ntype[g * 512:g * 512 + valid].rearrange("(o n) -> o n", o=1).to_broadcast([P, valid])), nt_free[s], *done)
        if valid < n * P:
            dve.need(nt_free[s], *done)
            tm = dve.mark(V.memset(ntr2[s][:, valid:n * P], 0))
            dve.need(tm)

    ta_ = [load_small(Wa[:, t, :, :], aW[t].rearrange("(c p) n -> p c n", p=P), *done) for t in range(T)]
    load_group(0)
    load_group(1)
    t_wr = [load_small(brP, br.rearrange("(o n) -> o n", o=1).to_broadcast([P, 1])),
            load_small(wrrow, wr.rearrange("n o -> o n").to_broadcast([P, C]), *done)]
    tf_ = [load_small(F1, fw1.rearrange("(c p) n -> p c n", p=P), *done),
           load_small(F2, fw2.rearrange("(c p) n -> p c n", p=P), *done),
           load_small(fb2row, fb2.rearrange("(o n) -> o n", o=1).to_broadcast([P, C]), *done),
           load_small(fb1T, fb1.rearrange("(c p) -> p c", p=P))]
    dve.need(*done)
    act.need(*done)

    def average(g):
        ts = tiles_of(g)
        n = len(ts)
        t = dve.mark(V.tensor_scalar(rden[:, 0:n, :], accv[:, ts[0]:ts[0] + n, C:AW], 0.5, None, ALU.max))
        dve.need(t)
        t = dve.mark(V.reciprocal(rden[:, 0:n, :], rden[:, 0:n, :]))
        dve.need(t, ag_free[g % 2])
        for i4 in range(n):
            t = dve.mark(V.tensor_tensor(out=ag[g % 2][:, i4, :].rearrange("p (h d) -> p h d", h=H),
                                         in0=accv[:, ts[i4], 0:C].rearrange("p (h d) -> p h d", h=H),
                                         in1=rden[:, i4, :].unsqueeze(2).to_broadcast([P, H, DK]), op=ALU.mult))
        return t

    t_ag, t_ma, t_x1, t_wS, pair_read = {}, {}, {}, [None], [None] * 2

    def split_types(tile):
        g, i4 = divmod(tile, GT)
        s = tile % NMA
        pe.need(t_ag[g])
        k, bank = ALLB.take(pe)
        for c in range(CC):
            ins = transpose(bank[:, c * P:(c + 1) * P], ag[g % 2][:, i4, c * P:(c + 1) * P])
        ag_free[g % 2] = tp = pe.mark(ins)
        act.need(tp, ma_free[s])
        ta2 = ALLB.free[k] = act.mark(A.copy(aT[s], bank[:, 0:C].rearrange("p (c n) -> p c n", c=CC)))
        dve.need(ta2, s_nt2[g % 2].last, ma_free[s])
        for ty in range(T):
            tm = dve.mark(V.scalar_tensor_tensor(
                out=MA[s][:, ty, :, :], in0=ntr2[g % 2][:, i4 * P:(i4 + 1) * P].unsqueeze(1).to_broadcast([P, CC, P]), scalar=float(ty),
                in1=aT[s], op0=ALU.is_equal, op1=ALU.mult))
        nt_free[g % 2] = t_ma[tile] = tm

    def finish_group(g):
        ts = tiles_of(g)
        n, s = len(ts), g % 2
        xb = x1[g % NX1]
        dve.need(t_x1[g])
        for i in range(n):
            t = dve.mark(V.bn_stats(stats[:, i, :], xb[:, i, :]))
        dve.need(t)
        for i in range(n):
            t = dve.mark(V.bn_aggr(mv[:, i, :], stats[:, i, :]))
        dve.need(t)
        t = dve.mark(V.tensor_scalar(var[:, 0:n], mv[:, 0:n, 1], LN_EPS, None, ALU.add))
        yield
        t = rsqrt(var[:, 0:n], rstd[:, 0:n], nt_tmp[:, 0:n], n, t)
        dve.need(t)
        t = dve.mark(V.scalar_tensor_tensor(out=shift[:, 0:n], in0=mv[:, 0:n, 0], scalar=-1.0, in1=rstd[:, 0:n], op0=ALU.mult, op1=ALU.mult))
        act.need(t, s_pair[s].last, pair_read[s])
        for i4 in range(n):
            t_xl = act.mark(A.activation(pair[s][:, i4, 0:C], xb[:, i4, :], ACT.Identity, bias=shift[:, i4:i4 + 1], scale=rstd[:, i4:i4 + 1]))
        pool.need(t_xl, s_out[s].last, s_pair[s].last)
        t = pool.mark(G.tensor_tensor(out=pair[s][:, 0:n, C:2 * C], in0=xb[:, 0:n, :], in1=pair[s][:, 0:n, 0:C], op=ALU.add))
        x1_free[g % NX1] = t
        s_pair[s].start(sp, lambda: nc.sync.dma_start(rows_of(d_pair, g), pair[s][:, 0:n, :]), t, t_xl)
        if g < NG - 1:
            s_out[s].start(sp, lambda: nc.sync.dma_start(rows_of(out, g), pair[s][:, 0:n, C:2 * C]), t)
        else:
            s_out[s].start(sp, lambda: nc.sync.dma_start(out[g * 512:N, :], pair[s][0:LAST, 0, C:2 * C]), t)
        yield
        t_wS[0] = router_weight(wS[:, ts[0]:ts[0] + n], [pair[s][:, i4, 0:C] for i4 in range(n)], t_xl)
        pair_read[s] = t_wS[0]
        yield

    xlT_free = [None]

    def turn_rows(src_, n, *tok):
        pe.need(*tok)
        for c in range(CC):
            k, bank = ALLB.take(pe)
            for i4 in range(n):
                ins = transpose(bank[:, i4 * P:(i4 + 1) * P], src_[:, i4, c * P:(c + 1) * P])
            tp = pe.mark(ins)
            act.need(tp, xlT_free[0])
            tt = ALLB.free[k] = act.mark(A.copy(xlT[:, c, 0:n * P], bank[:, 0:n * P]))
        return tt

    def router_weight(o, rows, tok):
        dve.need(tok, *t_wr)
        for i, r_ in enumerate(rows):
            t = dve.mark(V.scalar_tensor_tensor(out=wr_prod, in0=r_, scalar=1.0, in1=wrrow, op0=ALU.mult, op1=ALU.mult, accum_out=o[:, i:i + 1]))
            dve.need(t)
        return dve.mark(V.tensor_scalar(o, o, brP, None, ALU.add))

    t_ag[0] = average(0)
    split_types(0)
    split_types(1)
    pe.need(*ta_)
    finishing = iter(())
    for g in range(NG):
        for i4, tile in enumerate(tiles_of(g)):
            if i4 == 1 and g + 1 < NG:
                t_ag[g + 1] = average(g + 1)
            if tile + 2 < NT:
                split_types(tile + 2)
            pe.need(t_ma[tile])
            k, bank = ALLB.take(pe)
            for i in range(T * CC):
                ty, c = divmod(i, CC)
                ins = TE.matmul(bank[:, 0:C], lhsT=MA[tile % NMA][:, ty, c, :], rhs=Wa[:, ty, c, :], start=i == 0, stop=i == T * CC - 1)
            ma_free[tile % NMA] = tp = pe.mark(ins)
            next(finishing, None)
            dve.need(tp, s_b2[g % NX1].last, t_skn)
            t_x1[g] = ALLB.free[k] = dve.mark(V.scalar_tensor_tensor(
                out=x1[g % NX1][:, i4, :], in0=bank[:, 0:C], scalar=skn[:, tile:tile + 1], in1=x1[g % NX1][:, i4, :], op0=ALU.mult, op1=ALU.add))
        for _ in finishing:
            pass
        finishing = finish_group(g)
        if g + 2 < NG:
            load_group(g + 2)
    for _ in finishing:
        pass

    dve.need(t_wS[0])
    ki, hi_i, lo_i = key.bitcast(i32), khi.bitcast(i32), klo.bitcast(i32)
    t = dve.mark(V.tensor_scalar(ki, wS.bitcast(i32), 31, -2147483648, ALU.arith_shift_right, ALU.bitwise_or))
    dve.need(t)
    t = dve.mark(V.tensor_tensor(out=ki, in0=ki, in1=wS.bitcast(i32), op=ALU.bitwise_xor))
    dve.need(t)
    t = dve.mark(V.tensor_scalar(hi_i, ki, 16, None, ALU.logical_shift_right))
    t2 = dve.mark(V.tensor_scalar(lo_i, ki, 65535, None, ALU.bitwise_and))
    dve.need(t, t2)
    t = dve.mark(V.tensor_copy(khi, hi_i))
    t2 = dve.mark(V.tensor_copy(klo, lo_i))
    dve.need(t, t2)
    padm = tiny(1)
    t = dve.mark(V.tensor_scalar(padm, iota_p, float(LAST), None, ALU.is_lt))
    dve.need(t)
    for q in (khi, klo):
        t = dve.mark(V.tensor_scalar(q[:, NT - 1:NT], q[:, NT - 1:NT], 1.0, padm, ALU.add, ALU.mult))
        dve.need(t)
        t = dve.mark(V.tensor_scalar(q[:, NT - 1:NT], q[:, NT - 1:NT], 1.0, None, ALU.subtract))
        dve.need(t)

    def total(cols, tok):
        pe.need(tok)
        k, bank = ALLB.take(pe)
        tp = pe.mark(TE.matmul(bank[:, 0:cols.shape[1]], lhsT=ones, rhs=cols, start=True, stop=True))
        dve.need(tp)
        return k, bank

    def largest(src_, tok):
        dve.need(tok)
        t = dve.mark(V.memset(thr, 0.0))
        for bits in range(12, -1, -4):
            unit = float(1 << bits)
            dve.need(t)
            t = dve.mark(V.tensor_scalar(cand, iota_row[:, 1:RADIX], unit, thr, ALU.mult, ALU.add))
            dve.need(t)
            t = dve.mark(V.tensor_tensor(out=cmpv, in0=src_.unsqueeze(1).to_broadcast([P, RADIX - 1, NT]),
                                         in1=cand.unsqueeze(2).to_broadcast([P, RADIX - 1, NT]), op=ALU.is_ge))
            dve.need(t)
            t = dve.mark(V.tensor_reduce(cntp, cmpv, AX.X, ALU.add))
            k, bank = total(cntp, t)
            t = ALLB.free[k] = dve.mark(V.tensor_scalar(reach, bank[:, 0:RADIX - 1], float(KK), unit, ALU.is_ge, ALU.mult))
            dve.need(t)
            t = dve.mark(V.tensor_reduce(cand[:, 0:1], reach, AX.X, ALU.add))
            dve.need(t)
            t = dve.mark(V.tensor_tensor(out=thr, in0=thr, in1=cand[:, 0:1], op=ALU.add))
        return t

    t_tri = dve.mark(V.tensor_scalar(tri, iota_row, iota_p, None, ALU.is_gt))

    def count_before(o, mask, tok):
        pe.need(tok, t_tri)
        k, bank = ALLB.take(pe)
        TE.matmul(bank[:, 0:NT], lhsT=tri, rhs=mask, start=True, stop=True)
        tp = pe.mark(TE.matmul(bank[:, 64:64 + NT], lhsT=ones, rhs=mask, start=True, stop=True))
        dve.need(tp)
        t = dve.mark(V.tensor_copy(colt, bank[:, 64:64 + NT]))
        t2 = dve.mark(V.memset(o[:, 0:1], 0.0))
        dve.need(t)
        t = dve.mark(V.tensor_tensor_scan(out=o[:, 1:NT], data0=colt[:, 0:NT - 1], data1=colt[:, 0:NT - 1], initial=0.0, op0=ALU.add, op1=ALU.bypass))
        dve.need(t, t2)
        t = ALLB.free[k] = dve.mark(V.tensor_tensor(out=o, in0=o, in1=bank[:, 0:NT], op=ALU.add))
        return t

    t = largest(khi, t)
    dve.need(t)
    t = dve.mark(V.tensor_scalar(eqm, khi, thr, None, ALU.is_equal))
    dve.need(t)
    t = dve.mark(V.scalar_tensor_tensor(out=klo, in0=klo, scalar=1.0, in1=eqm, op0=ALU.add, op1=ALU.mult))
    t2 = dve.mark(V.tensor_scalar(cum, khi, thr, 65537.0, ALU.is_gt, ALU.mult))
    dve.need(t, t2)
    t = dve.mark(V.tensor_tensor(out=klo, in0=klo, in1=cum, op=ALU.add))
    dve.need(t)
    t = dve.mark(V.tensor_scalar(klo, klo, -1.0, None, ALU.add))
    t = largest(klo, t)
    dve.need(t)
    t = dve.mark(V.tensor_scalar(selv, klo, thr, None, ALU.is_gt))
    t_eq = dve.mark(V.tensor_scalar(eqm, klo, thr, None, ALU.is_equal))
    dve.need(t)
    t = dve.mark(V.tensor_reduce(cntp[:, 0:1], selv, AX.X, ALU.add))
    k, bank = total(cntp[:, 0:1], t)
    t_need = ALLB.free[k] = dve.mark(V.tensor_scalar(need_, bank[:, 0:1], -1.0, float(KK), ALU.mult, ALU.add))
    t = count_before(cum, eqm, t_eq)
    dve.need(t, t_need)
    t = dve.mark(V.scalar_tensor_tensor(out=eqm, in0=cum, scalar=need_, in1=eqm, op0=ALU.is_lt, op1=ALU.mult))
    dve.need(t)
    t = dve.mark(V.tensor_tensor(out=selv, in0=selv, in1=eqm, op=ALU.add))
    t_nf = pool.mark(G.iota(node_f, [[P, NT]], base=0, channel_multiplier=1, allow_small_or_imprecise_dtypes=True))
    t = count_before(slot, selv, t)
    dve.need(t, t_nf)
    t = dve.mark(V.tensor_tensor(out=slot, in0=slot, in1=node_f, op=ALU.subtract))
    dve.need(t)
    t = dve.mark(V.tensor_scalar(slot, slot, float(KT * P), None, ALU.subtract))
    dve.need(t)
    t = dve.mark(V.tensor_tensor(out=slot, in0=slot, in1=selv, op=ALU.mult))
    dve.need(t)
    t = dve.mark(V.tensor_tensor(out=slot, in0=slot, in1=node_f, op=ALU.add))
    dve.need(t)
    t = dve.mark(V.tensor_scalar(slot_i, slot, float(KT * P), None, ALU.add))
    t_slot = split_slots(slot_i, slot.bitcast(i32), t)
    k, bank = ALLB.take(pe)
    inv = Inverse(inv_room, KT, iota_row, bank, pe, dve)
    for j in range(NT):
        t_inv = inv.add(j, slot_mod, slot_div, node_f, j == 0, j == NT - 1, t_slot, t_nf)
    act.need(t_inv)
    t_picked = ALLB.free[k] = act.mark(A.copy(picked, bank[:, 0:KT]))

    KG = -(-KT // GT)
    lo = 0
    pk = [view(lo + i * GT * 2 * C, GT * 2 * C, "p (t n) -> p t n", t=GT) for i in range(2)]; lo += 2 * GT * 2 * C
    NY = 3
    yb = [view(lo + i * C, C) for i in range(NY)]; lo += NY * C
    s_pk = [[Slot(nc, f"pk{i}_{j}") for j in range(GT)] for i in range(2)]
    s_y = [Slot(nc, f"y{i}") for i in range(NY)]
    stage6 = [q.last for q in s_pair + s_out]
    pk_free, h_free = [t_slot, t_slot], None

    def picked_of(g):
        return list(range(g * GT, min(KT, (g + 1) * GT)))

    def gather_picked(g):
        for i, j in enumerate(picked_of(g)):
            s_pk[g % 2][i].start(pool, lambda: G.indirect_dma_start(
                pk[g % 2][:, i, :], None, d_pair[:, :], bass.IndirectOffsetOnAxis(ap=picked[:, j:j + 1], axis=0)),
                t_picked, pk_free[g % 2], *stage6)

    gather_picked(0)
    pe.need(*tf_)
    act.need(*tf_)
    dve.need(*tf_)
    t_xlT = turn_rows(pk[0], len(picked_of(0)), *[q.last for q in s_pk[0]])
    for g in range(KG):
        js = picked_of(g)
        n, s = len(js), g % 2
        w = n * P
        if g + 1 < KG:
            gather_picked(g + 1)
        dve.need(*[q.last for q in s_pk[s]])
        t_w = router_weight(wsel[:, g * GT:g * GT + n], [pk[s][:, i, 0:C] for i in range(n)], pk_free[s])
        pe.need(t_xlT)
        for oc in range(FC):
            k, bank = ALLB.take(pe)
            for c in range(CC):
                ins = TE.matmul(bank[:, 0:w], lhsT=F1[:, c, oc * P:(oc + 1) * P], rhs=xlT[:, c, 0:w], start=c == 0, stop=c == CC - 1)
            tp = pe.mark(ins)
            act.need(tp, h_free)
            th = ALLB.free[k] = act.mark(A.activation(hF[:, oc, 0:w], bank[:, 0:w], ACT.Gelu_apprx_tanh, bias=fb1T[:, oc:oc + 1]))
        xlT_free[0] = tp
        if g + 1 < KG:
            t_xlT = turn_rows(pk[1 - s], len(picked_of(g + 1)), *[q.last for q in s_pk[1 - s]])
        pe.need(th)
        for i, j in enumerate(js):
            k, bank = ALLB.take(pe)
            for c in range(FC):
                ins = TE.matmul(bank[:, 0:C], lhsT=hF[:, c, i * P:(i + 1) * P], rhs=F2[:, c, :], start=c == 0, stop=c == FC - 1)
            tp = pe.mark(ins)
            y = yb[j % NY]
            dve.need(tp, t_w, s_y[j % NY].last)
            t = ALLB.free[k] = dve.mark(V.tensor_tensor(out=y, in0=bank[:, 0:C], in1=fb2row, op=ALU.add))
            dve.need(t)
            pk_free[s] = t = dve.mark(V.scalar_tensor_tensor(out=y, in0=y, scalar=wsel[:, j:j + 1], in1=pk[s][:, i, C:2 * C], op0=ALU.mult, op1=ALU.add))
            rows = P if j < KT - 1 else KLAST
            s_y[j % NY].start(pool, lambda: G.indirect_dma_start(
                out[:, :], bass.IndirectOffsetOnAxis(ap=picked[0:rows, j:j + 1], axis=0), y[0:rows, :], None), t)
        h_free = tp
    sp.need(*[q.last for q in s_y])


_INS = ["x", "src", "dst", "edge_type_8", "node_type_4", "L0_gnn_k_linears", "L0_gnn_q_linears", "L0_gnn_v_linears",
        "L0_gnn_a_linears", "L0_gnn_relation_att", "L0_gnn_relation_msg", "L0_gnn_relation_pri", "L0_gnn_skip",
        "L0_mix_Wq", "L0_mix_Wk", "L0_mix_Wv", "L0_mix_Wm", "L0_mix_W1", "L0_mix_W2", "L0_mix_g1", "L0_mix_b1",
        "L0_mix_g2", "L0_mix_b2", "L0_ffn_wr", "L0_ffn_br", "L0_ffn_w1", "L0_ffn_b1", "L0_ffn_w2", "L0_ffn_b2"]


def kernel(**inputs):
    import numpy as _np
    import concourse.bacc as _bacc
    from concourse.bass_utils import run_bass_kernel_spmd as _run

    nc = _bacc.Bacc("TRN2", target_bir_lowering=False, num_devices=1)
    arrays, args = {}, []
    for name in _INS:
        a = _np.ascontiguousarray(inputs[name])
        arrays["in_" + name] = a
        args.append(nc.dram_tensor("in_" + name, a.shape, mybir.dt.from_np(a.dtype), kind="ExternalInput").ap())
    o = nc.dram_tensor("out_x", (N, C), f32, kind="ExternalOutput").ap()
    build(nc, *args, o)
    r = _run(nc, [arrays], core_ids=[0])
    return r.results[0]["out_x"]
```
